# Optimizing a Trainium2 kernel written in Bass

```python
import numpy as np
import jax
import jax.numpy as jnp

def _softmax(x, axis=-1):
    return jax.nn.softmax(x, axis=axis)

def _gelu(x):
    return jax.nn.gelu(x, approximate=True)

def _silu(x):
    return jax.nn.silu(x)

def _sigmoid(x):
    return jax.nn.sigmoid(x)

def _layernorm(x, axis=-1, eps=1e-05):
    m = jnp.mean(x, axis=axis, keepdims=True)
    v = jnp.var(x, axis=axis, keepdims=True)
    return (x - m) / jnp.sqrt(v + eps)

def _scatter_add(tgt, idx, src, axis=0):
    return tgt.at[idx].add(src)

def _segment_sum(src, seg, n):
    return jax.ops.segment_sum(src, seg, n)
kernel_name = 'mk_adj_ffn_d2_adj_r2_385560'

def setup_inputs(seed: int=0):
    np.random.seed(seed)
    _w = jnp.asarray

    def _rec_inputs():
        import jax
        import jax.numpy as jnp
        _gk = jax.random.key(seed)
        x = -0.0002928 + 1 * jax.random.normal(jax.random.fold_in(_gk, 1), (128, 128, 128), jnp.float32)
        _w = (1.0 + jnp.arange(128, dtype=jnp.float32)) ** (-0.5)
        _w = _w / _w.mean()
        _pij = jnp.clip(0.125 * _w[:, None] * _w[None, :], 0.0, 1.0)
        _a = jax.random.uniform(jax.random.fold_in(_gk, 2), (128, 128, 128)) < _pij
        adj = _a.astype(jnp.int32)
        return (x, adj)
    x, adj = _rec_inputs()

    def _L0_gnn_setup():
        import jax, jax.numpy as jnp
        import numpy as np
        NEG_BIG = -9000000000000000.0
        key = jax.random.key(seed)
        k1, k2, k3, k4 = jax.random.split(key, 4)
        B, N, F_in, F_out = (4, 2048, 128, 128)
        h = jax.random.normal(k1, (B, N, F_in), dtype=jnp.float32)
        adj = jax.random.randint(k2, (B, N, N), 0, 2, dtype=jnp.int32)
        bW = 1.414 * np.sqrt(6.0 / (F_in + F_out))
        W = jax.random.uniform(k3, (F_in, F_out), minval=-bW, maxval=bW, dtype=jnp.float32)
        ba = 1.414 * np.sqrt(6.0 / (2 * F_out + 1))
        a = jax.random.uniform(k4, (2 * F_out, 1), minval=-ba, maxval=ba, dtype=jnp.float32)
        return {'h': h, 'adj': adj, 'W': W, 'a': a}
    _L0_gnn_all = _L0_gnn_setup()
    _L0_gnn_in = {k: v for k, v in _L0_gnn_all.items() if k in ('W', 'a')}
    del _L0_gnn_all

    def _L0_ffn_setup():
        import jax, jax.numpy as jnp
        import numpy as np
        B, K, D = (256, 16, 128)
        E = 32
        H = int(D * 0.25)
        key = jax.random.key(seed)
        ks = jax.random.split(key, 7)
        d_rs = D ** (-0.5)
        h_rs = H ** (-0.5)
        x = jax.random.normal(ks[0], (B, K, D), dtype=jnp.float32)
        router_w = jax.random.uniform(ks[1], (E, D), jnp.float32, -d_rs, d_rs)
        router_b = jax.random.uniform(ks[2], (E,), jnp.float32, -d_rs, d_rs)
        W1 = jax.random.uniform(ks[3], (E, D, H), jnp.float32, -h_rs, h_rs)
        b1 = jax.random.uniform(ks[4], (E, H), jnp.float32, -h_rs, h_rs)
        W2 = jax.random.uniform(ks[5], (E, H, D), jnp.float32, -d_rs, d_rs)
        b2 = jax.random.uniform(ks[6], (E, D), jnp.float32, -d_rs, d_rs)
        return {'x': x, 'router_w': router_w, 'router_b': router_b, 'W1': W1, 'b1': b1, 'W2': W2, 'b2': b2}
    _L0_ffn_all = _L0_ffn_setup()
    _L0_ffn_in = {k: v for k, v in _L0_ffn_all.items() if k in ('router_w', 'router_b', 'W1', 'b1', 'W2', 'b2')}
    del _L0_ffn_all

    def _L1_gnn_setup():
        import jax, jax.numpy as jnp
        import numpy as np
        NEG_INF = -1000000000000.0
        ALPHA = 0.2
        key = jax.random.key(seed)
        k1, k2, k3, k4, k5 = jax.random.split(key, 5)
        B, N, Cin, Cout = (8, 1024, 128, 128)
        x = jax.random.normal(k1, (B, N, Cin), dtype=jnp.float32)
        mask = jax.random.randint(k2, (B, N, N), 0, 2, dtype=jnp.int32)
        W = jax.random.normal(k3, (Cout, Cin), dtype=jnp.float32) * Cin ** (-0.5)
        a = jax.random.normal(k4, (2, Cout), dtype=jnp.float32) * Cout ** (-0.5)
        bias = jax.random.normal(k5, (Cout,), dtype=jnp.float32)
        return {'x': x, 'mask': mask, 'W': W, 'a': a, 'bias': bias}
    _L1_gnn_all = _L1_gnn_setup()
    _L1_gnn_in = {k: v for k, v in _L1_gnn_all.items() if k in ('W', 'a', 'bias')}
    del _L1_gnn_all

    def _L1_ffn_setup():
        import jax, jax.numpy as jnp
        import numpy as np
        E, D, H, TOP_K = (6, 128, 128, 2)
        ROUTER_H = D // 2
        key = jax.random.key(seed)
        ks = jax.random.split(key, 12)
        s = 1.0 / np.sqrt(D)
        sh = 1.0 / np.sqrt(H)
        sr = 1.0 / np.sqrt(ROUTER_H)
        return {'features': jax.random.normal(ks[0], (8, 2048, D), dtype=jnp.float32), 'router_w1': jax.random.uniform(ks[1], (D, ROUTER_H), jnp.float32, -s, s), 'router_b1': jnp.zeros((ROUTER_H,), jnp.float32), 'router_w2': jax.random.uniform(ks[2], (ROUTER_H, E), jnp.float32, -sr, sr), 'router_b2': jnp.zeros((E,), jnp.float32), 'expert_w1': jax.random.uniform(ks[3], (E, D, H), jnp.float32, -s, s), 'expert_b1': jnp.zeros((E, H), jnp.float32), 'expert_w2': jax.random.uniform(ks[4], (E, H, H), jnp.float32, -sh, sh), 'expert_b2': jnp.zeros((E, H), jnp.float32), 'expert_w3': jax.random.uniform(ks[5], (E, H, D), jnp.float32, -sh, sh), 'expert_b3': jnp.zeros((E, D), jnp.float32)}
    _L1_ffn_all = _L1_ffn_setup()
    _L1_ffn_in = {k: v for k, v in _L1_ffn_all.items() if k in ('router_w1', 'router_b1', 'router_w2', 'router_b2', 'expert_w1', 'expert_b1', 'expert_w2', 'expert_b2', 'expert_w3', 'expert_b3')}
    del _L1_ffn_all
    return {'x': x, 'adj': adj, 'L0_gnn_W': _L0_gnn_in['W'], 'L0_gnn_a': _L0_gnn_in['a'], 'L0_ffn_router_w': _L0_ffn_in['router_w'], 'L0_ffn_router_b': _L0_ffn_in['router_b'], 'L0_ffn_W1': _L0_ffn_in['W1'], 'L0_ffn_b1': _L0_ffn_in['b1'], 'L0_ffn_W2': _L0_ffn_in['W2'], 'L0_ffn_b2': _L0_ffn_in['b2'], 'L1_gnn_W': _L1_gnn_in['W'], 'L1_gnn_a': _L1_gnn_in['a'], 'L1_gnn_bias': _L1_gnn_in['bias'], 'L1_ffn_router_w1': _L1_ffn_in['router_w1'], 'L1_ffn_router_b1': _L1_ffn_in['router_b1'], 'L1_ffn_router_w2': _L1_ffn_in['router_w2'], 'L1_ffn_router_b2': _L1_ffn_in['router_b2'], 'L1_ffn_expert_w1': _L1_ffn_in['expert_w1'], 'L1_ffn_expert_b1': _L1_ffn_in['expert_b1'], 'L1_ffn_expert_w2': _L1_ffn_in['expert_w2'], 'L1_ffn_expert_b2': _L1_ffn_in['expert_b2'], 'L1_ffn_expert_w3': _L1_ffn_in['expert_w3'], 'L1_ffn_expert_b3': _L1_ffn_in['expert_b3']}

def reference(x, adj, L0_gnn_W, L0_gnn_a, L0_ffn_router_w, L0_ffn_router_b, L0_ffn_W1, L0_ffn_b1, L0_ffn_W2, L0_ffn_b2, L1_gnn_W, L1_gnn_a, L1_gnn_bias, L1_ffn_router_w1, L1_ffn_router_b1, L1_ffn_router_w2, L1_ffn_router_b2, L1_ffn_expert_w1, L1_ffn_expert_b1, L1_ffn_expert_w2, L1_ffn_expert_b2, L1_ffn_expert_w3, L1_ffn_expert_b3):
    import jax
    import jax.numpy as jnp

    def _L0_gnn_ref(h, adj, W, a):
        import jax, jax.numpy as jnp
        import numpy as np
        NEG_BIG = -9000000000000000.0
        F_out = W.shape[1]
        Wh = jnp.einsum('bnf,fo->bno', h, W)
        src = Wh @ a[:F_out, 0]
        dst = Wh @ a[F_out:, 0]
        e = jax.nn.leaky_relu(src[:, :, None] + dst[:, None, :], negative_slope=0.2)
        scores = jnp.where(adj > 0, e, jnp.float32(NEG_BIG))
        attention = jax.nn.softmax(scores, axis=2)
        h_prime = jnp.einsum('bij,bjo->bio', attention, Wh)
        return jax.nn.relu(h_prime)

    def _L0_ffn_ref(x, router_w, router_b, W1, b1, W2, b2):
        import jax, jax.numpy as jnp
        import numpy as np
        B, K, D = (256, 16, 128)
        E = 32
        H = int(D * 0.25)
        xf = x.reshape(-1, D)
        logits = xf @ router_w.T + router_b
        idx = jnp.argmax(logits, axis=-1)
        w1t = jnp.take(W1, idx, axis=0)
        h = jnp.einsum('nd,ndh->nh', xf, w1t) + jnp.take(b1, idx, axis=0)
        h = jax.nn.relu(h)
        w2t = jnp.take(W2, idx, axis=0)
        out = jnp.einsum('nh,nhd->nd', h, w2t) + jnp.take(b2, idx, axis=0)
        out = jax.nn.relu(out)
        return out.reshape(x.shape)

    def _L1_gnn_ref(x, mask, W, a, bias):
        import jax, jax.numpy as jnp
        import numpy as np
        NEG_INF = -1000000000000.0
        ALPHA = 0.2
        hidden = jnp.einsum('bni,oi->bno', x, W)
        av = jnp.einsum('bno,ko->bnk', hidden, a)
        attn1, attn2 = (av[..., 0], av[..., 1])
        attn = attn1[:, :, None] + attn2[:, None, :]
        attn = jax.nn.leaky_relu(attn, negative_slope=ALPHA)
        attn = jnp.where(mask > 0, attn, attn + NEG_INF)
        attn = jax.nn.softmax(attn, axis=-1)
        out = jnp.einsum('bnm,bmo->bno', attn, hidden) + bias
        return out

    def _L1_ffn_ref(features, router_w1, router_b1, router_w2, router_b2, expert_w1, expert_b1, expert_w2, expert_b2, expert_w3, expert_b3):
        import jax, jax.numpy as jnp
        import numpy as np
        E, D, H, TOP_K = (6, 128, 128, 2)
        ROUTER_H = D // 2
        rh = jax.nn.relu(features @ router_w1 + router_b1)
        expert_logits = jax.nn.softmax(rh @ router_w2 + router_b2, axis=-1)
        top_w, top_i = jax.lax.top_k(expert_logits, TOP_K)
        routing_weights = jax.nn.softmax(top_w, axis=-1)
        h1 = jax.nn.relu(jnp.einsum('bsd,edh->bseh', features, expert_w1) + expert_b1)
        h2 = jax.nn.relu(jnp.einsum('bseh,ehf->bsef', h1, expert_w2) + expert_b2)
        expert_out = jnp.einsum('bsef,efo->bseo', h2, expert_w3) + expert_b3
        sel = jnp.take_along_axis(expert_out, top_i[:, :, :, None], axis=2)
        combined = jnp.sum(sel * routing_weights[..., None], axis=2)
        return combined
    x = x + _L0_gnn_ref(_layernorm(x, axis=-1), adj, L0_gnn_W, L0_gnn_a)
    x = x + _L0_ffn_ref(_layernorm(x, axis=-1), L0_ffn_router_w, L0_ffn_router_b, L0_ffn_W1, L0_ffn_b1, L0_ffn_W2, L0_ffn_b2)
    x = x + _L1_gnn_ref(_layernorm(x, axis=-1), adj, L1_gnn_W, L1_gnn_a, L1_gnn_bias)
    x = x + _L1_ffn_ref(_layernorm(x, axis=-1), L1_ffn_router_w1, L1_ffn_router_b1, L1_ffn_router_w2, L1_ffn_router_b2, L1_ffn_expert_w1, L1_ffn_expert_b1, L1_ffn_expert_w2, L1_ffn_expert_b2, L1_ffn_expert_w3, L1_ffn_expert_b3)
    return x

_drawn_inputs = setup_inputs


def setup_inputs(seed=0):
    import zlib

    import numpy as np

    out = dict(_drawn_inputs(seed))
    spreads = {'L1_ffn_router_b1': (0.0, 0.1),
     'L1_ffn_router_b2': (0.0, 0.361),
     'L1_ffn_expert_b1': (0.0, 0.8),
     'L1_ffn_expert_b2': (0.0, 0.448),
     'L1_ffn_expert_b3': (0.0, 0.1)}
    factors = {'L0_ffn_b1': 5.102}
    for name, (base, spread) in spreads.items():
        noise = np.random.default_rng([zlib.crc32(name.encode()), seed]).standard_normal(out[name].shape)
        drawn = base * np.exp(spread * noise) if base else spread * noise
        out[name] = jnp.asarray(drawn.astype(out[name].dtype))
    for name, factor in factors.items():
        out[name] = (out[name] * factor).astype(out[name].dtype)
    return out
```

```python
from contextlib import ExitStack

import concourse.bass as bass
from concourse import mybir

F32 = mybir.dt.float32
F32R = mybir.dt.float32r
BF16 = mybir.dt.bfloat16
I32 = mybir.dt.int32
ALU = mybir.AluOpType
ACT = mybir.ActivationFunctionType
AX_X = mybir.AxisListType.X

NEG_BIG = -9000000000000000.0
SLOPE = 0.2
EPS = 1e-5
UNSELECTED = -1e30

LAG = {"g0": 0, "p0": 0, "f0": 1, "g1": 1, "p1": 1, "f1": 2}
DEPTH = max(LAG.values())

ORDER = [
    ("f0", "hold"), ("g1", "hold"), ("f1", "hold"),
    ("f0", "chunk0"), ("g0", "norm"), ("f0", "chunk1"), ("g0", "flip"), ("f0", "chunk2"),
     ("g0", "project"), ("f0", "chunk3"), ("g0", "row"), ("f0", "chunk4"), ("g0", "scores"),
     ("f0", "chunk5"), ("g0", "softmax"), ("f0", "chunk6"), ("g0", "flip_probs"), ("f0", "chunk7"),
     ("g0", "mix"), ("f0", "chunk8"), ("p0", "norm"), ("f0", "chunk9"), ("f0", "tail"),
     ("f1", "up0"), ("p0", "flip"), ("f1", "up1"), ("g1", "norm"), ("f1", "mid0"), ("p0", "route"),
     ("f1", "up2"), ("p0", "spread"), ("f1", "mid1"), ("g1", "flip"), ("f1", "down0"),
     ("g1", "project"), ("f1", "up3"), ("f1", "mid2"), ("g1", "row"), ("f1", "down1"),
     ("g1", "scores"), ("f1", "up4"), ("f1", "mid3"), ("g1", "softmax"), ("f1", "down2"),
     ("f1", "up5"), ("g1", "flip_probs"), ("f1", "mid4"), ("f1", "down3"), ("g1", "mix"),
     ("f1", "mid5"), ("p1", "norm"), ("f1", "down4"), ("p1", "flip"), ("f1", "down5"),
     ("p1", "hidden"), ("f1", "tail"), ("p1", "route"), ("p1", "spread")]


def four_layer_kernel(nc, x, adj, g0_w, g0_w_turned, g0_a, g1_w, g1_w_turned, g1_a, g1_bias,
                      f0_router, f0_router_b, f0_w1, f0_b1, f0_w2, f0_b2,
                      f1_router1, f1_router1_b, f1_router2, f1_router2_b,
                      f1_w1, f1_b1, f1_w2, f1_b2, f1_w3, f1_b3,
                      eye, rank0, rank1, gate_pick, out):
    B, N, D = x.shape
    P = 128
    assert N == P and D == P
    GB = 4
    T = GB * N
    GROUPS = B // GB
    E0 = f0_router.shape[1]
    CH = f0_w1.shape[1] // P
    R1 = f1_router1.shape[1]
    E1 = f1_router2.shape[1]
    KR = 32
    REP = P // KR
    PARTS = 3

    ctx = ExitStack()
    with ctx:
        def sb(name, shape, dt=F32):
            return ctx.enter_context(nc.sbuf_tensor(name, shape, dt))

        def sem(name):
            return ctx.enter_context(nc.semaphore(name))

        hid_bank = [ctx.enter_context(nc.psum_tensor(f"hid_bank{i}", [P, T], F32)) for i in range(3)]
        out_bank = ctx.enter_context(nc.psum_tensor("out_bank", [P, T], F32))
        gate_bank = ctx.enter_context(nc.psum_tensor("gate_bank", [P, T], F32))
        flip_bank = ctx.enter_context(nc.psum_tensor("flip_bank", [P, T], F32))
        score_bank = ctx.enter_context(nc.psum_tensor("score_bank", [P, T], F32))
        value_bank = ctx.enter_context(nc.psum_tensor("value_bank", [P, T], F32))
        flip16 = flip_bank[:, :].bitcast(BF16)

        ident = sb("ident", [P, P])
        ident16 = sb("ident16", [P, P], BF16)
        ones16 = sb("ones16", [KR, P], BF16)
        minus_half = sb("minus_half", [P, GB])
        eps_sb = sb("eps_sb", [P, GB])
        one_sb = sb("one_sb", [P, 1])
        rank0_sb = sb("rank0_sb", [P, E0])
        rank1_sb = sb("rank1_sb", [P, E1])
        pick_f32 = sb("pick_f32", [P, E1, P])
        pick16 = sb("pick16", [P, E1, P], BF16)
        bias_g1 = sb("bias_g1", [P, D])
        rt0 = sb("rt0", [P, E0])
        rt0_b = sb("rt0_b", [P, E0])
        rt1_b = sb("rt1_b", [P, 1])
        rt2 = sb("rt2", [P, E1])
        rt2_b = sb("rt2_b", [P, E1])
        b1_f1 = sb("b1_f1", [P, E1])
        b2_f1 = sb("b2_f1", [P, E1])
        split_sources = {
            "w1_f0": (CH * P, f0_w1), "w2_f0": (CH * P, f0_w2.rearrange("(c p) d -> p c d", p=P)),
            "rt1": (R1, f1_router1), "w1_f1": (E1 * P, f1_w1), "w2_f1": (E1 * P, f1_w2),
            "w3_f1": (E1 * P, f1_w3)}
        raw, hi, lo = {}, {}, {}
        for name, (cols, _) in split_sources.items():
            raw[name] = sb(f"{name}_raw", [P, cols])
            hi[name] = sb(f"{name}_hi", [P, cols], F32R)
            lo[name] = sb(f"{name}_lo", [P, cols], F32R)
        bias_raw = {"b1_f0": sb("b1_f0_raw", [P, CH * P]), "b2_f0": sb("b2_f0_raw", [P, D]),
                    "b3_f1": sb("b3_f1_raw", [P, D])}
        bias16 = {"b1_f0": sb("b1_f0_16", [P, CH * P], BF16), "b2_f0": sb("b2_f0_16", [P, D], BF16),
                  "b3_f1": sb("b3_f1_16", [P, D], BF16)}
        part_tmp = sb("part_tmp", [P, CH * P], BF16)

        x0 = sb("x0", [P, GB, D])
        x1 = sb("x1", [P, GB, D])
        x1_held = sb("x1_held", [P, GB, D])
        x2 = sb("x2", [P, GB, D])
        x2_bias = sb("x2_bias", [P, GB, D])
        x3 = sb("x3", [P, GB, D])
        x3_held = sb("x3_held", [P, GB, D])
        x4 = sb("x4", [P, GB, D])
        adj_sb = sb("adj_sb", [P, GB, N], I32)


        norm = {}
        for k, src in (("g0", x0), ("p0", x1), ("g1", x2), ("p1", x3)):
            norm[k] = dict(
                src=src, stats=sb(f"{k}_stats", [P, GB, 6]), mean_var=sb(f"{k}_mean_var", [P, GB, 2]),
                var_eps=sb(f"{k}_var_eps", [P, GB]), rstd=sb(f"{k}_rstd", [P, GB]),
                normed=sb(f"{k}_normed", [P, GB, D]),
                **{s: sem(f"{k}_{s}") for s in ("stats_done", "var_ready", "eps_added", "rstd_ready",
                                                "normed_ready", "flipped")})

        gnn = {}
        for k, w, w_turned, a in (("g0", g0_w, g0_w_turned, g0_a), ("g1", g1_w, g1_w_turned, g1_a)):
            gnn[k] = dict(
                w_dram=w, w_turned_dram=w_turned, a_dram=a,
                w=sb(f"{k}_w", [P, D]),
                w_turned=sb(f"{k}_w_turned", [P, D]),
                a=sb(f"{k}_a", [P, 2]),
                score_w=sb(f"{k}_score_w", [P, 2]),
                masked=sb(f"{k}_masked", [P, T], BF16),
                normed_t=sb(f"{k}_normed_t", [P, T]),
                values=sb(f"{k}_values", [P, T]),
                src_dst=sb(f"{k}_src_dst", [P, GB, 2]),
                rest1=sb(f"{k}_rest1", [P, GB]), rest2=sb(f"{k}_rest2", [P, GB]),
                dst_parts=sb(f"{k}_dst_parts", [P, GB, KR], BF16),
                dst_rows=sb(f"{k}_dst_rows", [KR, T], BF16),
                scores=sb(f"{k}_scores", [P, GB, N]), leaky=sb(f"{k}_leaky", [P, GB, N]),
                neg_max=sb(f"{k}_neg_max", [P, GB]), neg_leaky_max=sb(f"{k}_neg_leaky_max", [P, GB]),
                probs=sb(f"{k}_probs", [P, GB, N]), row_sum=sb(f"{k}_row_sum", [P, GB]),
                row_rcp=sb(f"{k}_row_rcp", [P, GB]), probs_t=sb(f"{k}_probs_t", [P, T]),
                **{s: sem(f"{k}_{s}") for s in (
                    "mask_ready", "normed_t_ready", "src_dst_done", "values_done", "src_dst_ready",
                    "part1_ready", "rest1_ready", "part2_ready", "rest2_ready", "dst_parts_ready",
                    "rows_flipped", "rows_ready", "scores_done", "values_ready", "scores_ready",
                    "neg_max_ready", "neg_leaky_max_ready", "leaky_ready", "probs_ready",
                    "row_rcp_ready", "probs_flipped", "probs_t_ready", "mixed", "x_ready")})
        mixed_relu = sb("mixed_relu", [P, GB, D])
        mixed_relu_ready = sem("mixed_relu_ready")
        x2_bias_ready = sem("x2_bias_ready")
        x1_held_ready = sem("x1_held_ready")
        x3_held_ready = sem("x3_held_ready")

        p0 = dict(
            hi=sb("p0_hi", [P, T], F32R), lo=sb("p0_lo", [P, T], F32R),
            logits=sb("p0_logits", [P, GB, E0]), top=sb("p0_top", [P, GB]),
            at_top=sb("p0_at_top", [P, GB, E0]), ranked=sb("p0_ranked", [P, GB, E0]),
            first=sb("p0_first", [P, GB]), onehot=sb("p0_onehot", [P, GB, REP, E0], BF16),
            spread=sb("p0_spread", [P, T], BF16),
            link=sem("p0_link"), LINKS=5,
            **{s: sem(f"p0_{s}") for s in ("hi_ready", "lo_ready", "logits_done", "onehot_ready",
                                           "spread_flipped", "spread_ready")})
        p1 = dict(
            hi=sb("p1_hi", [P, T], F32R), lo=sb("p1_lo", [P, T], F32R), hidden=sb("p1_hidden", [P, T]),
            t6={s: sb(f"p1_{s}", [P, GB, E1]) for s in (
                "logits", "shifted", "exps", "probs", "at_top", "ranked", "first", "others", "at_second",
                "ranked2", "second", "gate1", "gate2", "gates", "rest1", "rest2")},
            t1={s: sb(f"p1_{s}", [P, GB]) for s in (
                "neg_max", "sum", "rcp", "top", "rank_top", "next", "rank_next", "gap", "exp_gap",
                "gap_sum", "weight1", "weight2")},
            parts=sb("p1_parts", [P, GB, REP, KR], BF16),
            spread=sb("p1_spread", [P, T], BF16),
            link=sem("p1_link"), LINKS=26,
            **{s: sem(f"p1_{s}") for s in (
                "hi_ready", "lo_ready", "hidden_done", "hidden_ready", "logits_done", "shifted_ready",
                "exps_ready", "gap_ready", "exp_gap_ready", "parts_ready", "spread_flipped",
                "spread_ready")})

        f0 = dict(
            hi=[sb(f"f0_hi{i}", [P, T], F32R) for i in range(3)],
            lo=[sb(f"f0_lo{i}", [P, T], F32R) for i in range(3)], sum_t=sb("f0_sum_t", [P, T]),
            **{s: sem(f"f0_{s}") for s in (
                "up_done", "hi_ready", "lo_ready", "down_done", "sum_ready", "sum_flipped", "x_ready")})
        f1 = dict(
            relu1=[sb(f"f1_relu1_{i}", [P, T]) for i in range(2)],
            hi1=[sb(f"f1_hi1_{i}", [P, T], F32R) for i in range(2)],
            lo1=[sb(f"f1_lo1_{i}", [P, T], F32R) for i in range(2)],
            relu2=[sb(f"f1_relu2_{i}", [P, T]) for i in range(2)],
            gated=[sb(f"f1_gated_{i}", [P, T]) for i in range(2)],
            hi2=[sb(f"f1_hi2_{i}", [P, T], F32R) for i in range(2)],
            lo2=[sb(f"f1_lo2_{i}", [P, T], F32R) for i in range(2)],
            sum_t=sb("f1_sum_t", [P, T]),
            **{s: sem(f"f1_{s}") for s in (
                "up_done", "relu1_ready", "hi1_ready", "lo1_ready", "gate_done", "mid_done",
                "relu2_ready", "gated_ready", "hi2_ready", "lo2_ready", "down_done",
                "sum_ready", "sum_flipped", "x_ready")})

        weights_in = sem("weights_in")
        x_in = sem("x_in")
        adj_in = sem("adj_in")
        x_out = sem("x_out")
        fills_done = sem("fills_done")
        hi_split = sem("hi_split")
        setup_link = sem("setup_link")
        picked = sem("picked")
        score_w_done = sem("score_w_done")
        setup_ready = sem("setup_ready")

        plain_loads = [
            (ident, eye), (rank0_sb, rank0), (rank1_sb, rank1), (pick_f32, gate_pick),
            (bias_g1, g1_bias.partition_broadcast(P)), (rt0, f0_router),
            (rt0_b, f0_router_b.partition_broadcast(P)), (rt1_b, f1_router1_b), (rt2, f1_router2),
            (rt2_b, f1_router2_b.partition_broadcast(P)), (b1_f1, f1_b1), (b2_f1, f1_b2),
            (bias_raw["b1_f0"], f0_b1.partition_broadcast(P)), (bias_raw["b2_f0"], f0_b2),
            (bias_raw["b3_f1"], f1_b3)]
        for k in ("g0", "g1"):
            q = gnn[k]
            plain_loads += [(q["w"], q["w_dram"]), (q["w_turned"], q["w_turned_dram"]), (q["a"], q["a_dram"])]
        LOADS = 16 * (len(plain_loads) + len(split_sources))
        NSPLIT = len(split_sources)

        x_groups = x.rearrange("(g b) n d -> g n b d", b=GB)
        adj_groups = adj.rearrange("(g b) n m -> g n b m", b=GB)
        out_groups = out.rearrange("(g b) n d -> g n b d", b=GB)

        def per_graph(tile, b, width=N):
            return tile[:, b * width:(b + 1) * width]

        def flat(tile):
            return tile[:, :, :].rearrange("p b n -> p (b n)")

        def wide(column, width):
            return column[:, :].unsqueeze(2).broadcast_to([P, GB, width])

        def every_graph(row, width):
            return row[:, :].unsqueeze(1).broadcast_to([P, GB, width])

        def nth(g, i, n):
            return g * n + (i + 1)

        def earlier(eng, signal, g, back=1, i=0, n=1):
            if not isinstance(g, int) or g >= back:
                eng.wait_ge(signal, nth(g - back, i, n))

        def ahead(g, by):
            return min(g + by + 1, GROUPS) if isinstance(g, int) else g + by + 1

        def apart(eng):
            eng.wait_ge(fills_done, 1)

        def run(eng, pieces):
            def step(t, inside):
                for stage, piece in ORDER:
                    g = t - LAG[stage]
                    if (inside or 0 <= g < GROUPS) and (stage, piece) in pieces:
                        pieces[stage, piece](g)
            for t in range(DEPTH + 1):
                step(t, False)
            with eng.Fori(DEPTH + 1, GROUPS) as t:
                step(t, True)
            for t in range(GROUPS, GROUPS + DEPTH):
                step(t, False)

        block = ctx.enter_context(nc.Block())

        @block.sync
        def _(sp):
            sp.dma_start(x0[:, :, :], x_groups[0]).then_inc(x_in, 16)
            sp.dma_start(adj_sb[:, :, :], adj_groups[0]).then_inc(adj_in, 16)
            for tile, src in plain_loads:
                dst = tile[:, :, :] if len(tile.shape) == 3 else tile[:, :]
                sp.dma_start(dst, src).then_inc(weights_in, 16)
            for name, (_, src) in split_sources.items():
                dst = raw[name][:, :]
                if len(src.shape) == 3:
                    dst = dst.rearrange("p (c d) -> p c d", d=src.shape[2])
                sp.dma_start(dst, src).then_inc(weights_in, 16)

            def load_next(g):
                sp.wait_ge(gnn["g0"]["mask_ready"], g)
                sp.dma_start(adj_sb[:, :, :], adj_groups[g]).then_inc(adj_in, 16)
                sp.wait_ge(gnn["g0"]["x_ready"], g)
                sp.dma_start(x0[:, :, :], x_groups[g]).then_inc(x_in, 16)

            def store(g):
                sp.wait_ge(f1["x_ready"], g + 1)
                sp.dma_start(out_groups[g], x4[:, :, :]).then_inc(x_out, 16)

            load_next(1)
            load_next(2)
            with sp.Fori(3, GROUPS) as g:
                store(g - 3)
                load_next(g)
            for g in range(GROUPS - 3, GROUPS):
                store(g)
            sp.wait_ge(x_out, 16 * GROUPS)

        @block.gpsimd
        def _(pool):
            nc.gpsimd.memset(ones16[:, :], 1.0)
            nc.gpsimd.memset(minus_half[:, :], -0.5)
            nc.gpsimd.memset(eps_sb[:, :], EPS)
            nc.gpsimd.memset(one_sb[:, :], 1.0)
            nc.gpsimd.memset(p1["parts"][:, :, :, :], 0.0)
            for k in ("g0", "g1"):
                nc.gpsimd.memset(gnn[k]["dst_parts"][:, :, :], 0.0)
            nc.gpsimd.memset(bias16["b2_f0"][:, :], 0.0)
            nc.gpsimd.memset(bias16["b3_f1"][:, :], 0.0)
            nc.gpsimd.memset(bias16["b1_f0"][:, :], 0.0).then_inc(fills_done, 1)
            pool.wait_ge(fills_done, 1)
            pool.wait_ge(setup_ready, 1)
            for r in range(PARTS):
                v = bias16["b1_f0"][KR * r:KR * (r + 1), :].rearrange("p (e h) -> p e h", e=E0)
                nc.gpsimd.affine_select(out=v, in_=v, compare_op=ALU.is_equal,
                                        fill=UNSELECTED if r == 0 else 0.0, base=0,
                                        pattern=[[-1, E0], [0, CH * P // E0]],
                                        channel_multiplier=1).then_inc(picked, 1)
            pool.wait_ge(picked, PARTS)

            def normalise(k):
                q = norm[k]

                def piece(g):
                    pool.wait_ge(q["var_ready"], g + 1)
                    nc.gpsimd.tensor_tensor(q["var_eps"][:, :], q["mean_var"][:, :, 1], eps_sb[:, :],
                                            ALU.add).then_inc(q["eps_added"], 1)
                    pool.wait_ge(q["eps_added"], g + 1)
                    nc.gpsimd.tensor_tensor(q["rstd"][:, :], q["var_eps"][:, :], minus_half[:, :],
                                            ALU.pow).then_inc(q["rstd_ready"], 1)
                    apart(pool)
                    pool.wait_ge(q["rstd_ready"], g + 1)
                    earlier(pool, q["flipped"], g)
                    for b in range(GB):
                        last = nc.gpsimd.tensor_scalar(q["normed"][:, b, :], q["src"][:, b, :],
                                                       q["mean_var"][:, b, 0:1], q["rstd"][:, b:b + 1],
                                                       ALU.subtract, ALU.mult)
                    last.then_inc(q["normed_ready"], 1)
                    if k == "g1":
                        earlier(pool, gnn["g1"]["x_ready"], g)
                        nc.gpsimd.tensor_tensor(x2_bias[:, :, :], x2[:, :, :], every_graph(bias_g1, D),
                                                ALU.add).then_inc(x2_bias_ready, 1)
                return piece

            def add_mixed(g):
                pool.wait_ge(mixed_relu_ready, g + 1)
                nc.gpsimd.tensor_tensor(flat(x1), flat(x0), flat(mixed_relu),
                                        ALU.add).then_inc(gnn["g0"]["x_ready"], 1)

            def hold_x1(g):
                earlier(pool, f0["x_ready"], g)
                pool.wait_ge(gnn["g0"]["x_ready"], g + 1)
                nc.gpsimd.tensor_tensor(flat(x1_held), flat(x1), one_sb[:, :].broadcast_to([P, T]),
                                        ALU.mult).then_inc(x1_held_ready, 1)

            def hold_x3(g):
                earlier(pool, f1["x_ready"], g)
                pool.wait_ge(gnn["g1"]["x_ready"], g + 1)
                nc.gpsimd.tensor_tensor(flat(x3_held), flat(x3), one_sb[:, :].broadcast_to([P, T]),
                                        ALU.mult).then_inc(x3_held_ready, 1)

            def hold_mask(g):
                apart(pool)
                earlier(pool, gnn["g1"]["scores_done"], g)
                pool.wait_ge(gnn["g0"]["mask_ready"], g + 1)
                nc.gpsimd.tensor_copy(gnn["g1"]["masked"][:, :], gnn["g0"]["masked"][:, :])\
                    .then_inc(gnn["g1"]["mask_ready"], 1)

            run(pool, {("f1", "hold"): hold_x3, ("f0", "hold"): hold_x1, ("g1", "hold"): hold_mask,
                       ("g0", "norm"): normalise("g0"), ("g0", "mix"): add_mixed,
                       ("p0", "norm"): normalise("p0"), ("g1", "norm"): normalise("g1"),
                       ("p1", "norm"): normalise("p1")})

        @block.scalar
        def _(act):
            act.wait_ge(weights_in, LOADS)
            for name in split_sources:
                nc.scalar.activation(hi[name][:, :], raw[name][:, :], ACT.Copy).then_inc(hi_split, 1)

            def gnn_flip(k):
                q = gnn[k]

                def piece(g):
                    act.wait_ge(norm[k]["flipped"], g + 1)
                    earlier(act, q["values_done"], g)
                    nc.scalar.activation(q["normed_t"][:, :], flip_bank[:, :], ACT.Copy)\
                        .then_inc(q["normed_t_ready"], 1)
                return piece

            def gnn_project(k):
                q = gnn[k]

                def piece(g):
                    act.wait_ge(q["values_done"], g + 1)
                    earlier(act, q["mixed"], g)
                    nc.scalar.activation(q["values"][:, :], value_bank[:, :], ACT.Copy)\
                        .then_inc(q["values_ready"], 1)
                return piece

            def gnn_scores(k):
                q = gnn[k]

                def piece(g):
                    act.wait_ge(q["scores_done"], g + 1)
                    act.wait_ge(q["src_dst_ready"], g + 1)
                    earlier(act, q["leaky_ready"], g)
                    for b in range(GB):
                        last = nc.scalar.activation(q["scores"][:, b, :], per_graph(score_bank, b),
                                                    ACT.Identity, bias=q["src_dst"][:, b, 0:1])
                    last.then_inc(q["scores_ready"], 1)
                return piece

            def gnn_softmax(k):
                q = gnn[k]

                def piece(g):
                    act.wait_ge(q["leaky_ready"], g + 1)
                    act.wait_ge(q["neg_leaky_max_ready"], g + 1)
                    earlier(act, q["probs_flipped"], g)
                    earlier(act, q["row_rcp_ready"], g)
                    for b in range(GB):
                        last = nc.scalar.activation(q["probs"][:, b, :], q["leaky"][:, b, :], ACT.Exp,
                                                    bias=q["neg_leaky_max"][:, b:b + 1],
                                                    accum_out=q["row_sum"][:, b:b + 1])
                    last.then_inc(q["probs_ready"], 1)
                return piece

            def g0_mix(g):
                q = gnn["g0"]
                act.wait_ge(q["mixed"], g + 1)
                act.wait_ge(q["row_rcp_ready"], g + 1)
                earlier(act, q["x_ready"], g)
                for b in range(GB):
                    last = nc.scalar.activation(mixed_relu[:, b, :], per_graph(value_bank, b), ACT.Relu,
                                                scale=q["row_rcp"][:, b:b + 1])
                last.then_inc(mixed_relu_ready, 1)

            def p_flip(k, p, last_read, n):
                def piece(g):
                    act.wait_ge(norm[k]["flipped"], g + 1)
                    earlier(act, last_read, g, 1, n - 1, n)
                    nc.scalar.activation(p["hi"][:, :], flip_bank[:, :], ACT.Copy).then_inc(p["hi_ready"], 1)
                return piece

            def p0_spread(g):
                act.wait_ge(p0["spread_flipped"], g + 1)
                earlier(act, f0["up_done"], g, 1, CH - 1, CH)
                nc.scalar.activation(p0["spread"][:, :], flip16[:, 0:T], ACT.Copy).then_inc(p0["spread_ready"], 1)

            def p1_hidden(g):
                act.wait_ge(p1["hidden_done"], g + 1)
                earlier(act, p1["logits_done"], g)
                nc.scalar.activation(p1["hidden"][:, :], score_bank[:, :], ACT.Relu,
                                     bias=rt1_b[:, 0:1]).then_inc(p1["hidden_ready"], 1)

            def p1_route(g):
                act.wait_ge(p1["shifted_ready"], g + 1)
                nc.scalar.activation(flat(p1["t6"]["exps"]), flat(p1["t6"]["shifted"]), ACT.Exp)\
                    .then_inc(p1["exps_ready"], 1)
                act.wait_ge(p1["gap_ready"], g + 1)
                nc.scalar.activation(p1["t1"]["exp_gap"][:, :], p1["t1"]["gap"][:, :], ACT.Exp)\
                    .then_inc(p1["exp_gap_ready"], 1)

            def p1_spread(g):
                act.wait_ge(p1["spread_flipped"], g + 1)
                earlier(act, f1["gate_done"], g, 1, E1 - 1, E1)
                nc.scalar.activation(p1["spread"][:, :], flip16[:, 0:T], ACT.Copy).then_inc(p1["spread_ready"], 1)

            def f0_chunk(c):
                def piece(g):
                    act.wait_ge(f0["up_done"], nth(g, c, CH))
                    if c >= 3:
                        act.wait_ge(f0["down_done"], nth(g, c - 3, CH))
                    else:
                        earlier(act, f0["down_done"], g, 1, CH - 1, CH)
                    nc.scalar.activation(f0["hi"][c % 3][:, :], hid_bank[c % 3][:, :], ACT.Relu)\
                        .then_inc(f0["hi_ready"], 1)
                return piece

            def f0_tail(g):
                act.wait_ge(f0["down_done"], nth(g, CH - 1, CH))
                earlier(act, f0["sum_flipped"], g)
                nc.scalar.activation(f0["sum_t"][:, :], out_bank[:, :], ACT.Relu).then_inc(f0["sum_ready"], 1)

            def f1_up(e):
                def piece(g):
                    if e >= 2:
                        f1_hi2(e - 2, g)
                    act.wait_ge(f1["up_done"], nth(g, e, E1))
                    if e >= 2:
                        act.wait_ge(f1["mid_done"], nth(g, e - 2, E1))
                    else:
                        earlier(act, f1["mid_done"], g, 1, E1 - 2 + e, E1)
                    bank = hid_bank[max(0, 2 * e - 1) % 3]
                    nc.scalar.activation(f1["relu1"][e % 2][:, :], bank[:, :], ACT.Relu,
                                         bias=b1_f1[:, e:e + 1]).then_inc(f1["relu1_ready"], 1)
                    nc.scalar.activation(f1["hi1"][e % 2][:, :], bank[:, :], ACT.Relu,
                                         bias=b1_f1[:, e:e + 1]).then_inc(f1["hi1_ready"], 1)
                return piece

            def f1_hi2(e, g):
                act.wait_ge(f1["gated_ready"], nth(g, e, E1))
                if e >= 2:
                    act.wait_ge(f1["down_done"], nth(g, e - 2, E1))
                else:
                    earlier(act, f1["down_done"], g, 1, E1 - 2 + e, E1)
                nc.scalar.activation(f1["hi2"][e % 2][:, :], f1["gated"][e % 2][:, :], ACT.Copy)\
                    .then_inc(f1["hi2_ready"], 1)

            def f1_mid(e):
                def piece(g):
                    act.wait_ge(f1["mid_done"], nth(g, e, E1))
                    if e >= 2:
                        act.wait_ge(f1["gated_ready"], nth(g, e - 2, E1))
                    else:
                        earlier(act, f1["gated_ready"], g, 1, E1 - 2 + e, E1)
                    nc.scalar.activation(f1["relu2"][e % 2][:, :], hid_bank[(2 * e + 2) % 3][:, :], ACT.Relu,
                                         bias=b2_f1[:, e:e + 1]).then_inc(f1["relu2_ready"], 1)
                return piece

            def f1_down(e):
                def piece(g):
                    if e >= E1 - 2:
                        f1_hi2(e, g)
                return piece

            def f1_tail(g):
                act.wait_ge(f1["down_done"], nth(g, E1 - 1, E1))
                earlier(act, f1["sum_flipped"], g)
                nc.scalar.activation(f1["sum_t"][:, :], out_bank[:, :], ACT.Copy).then_inc(f1["sum_ready"], 1)

            pieces = {("g0", "mix"): g0_mix, ("p0", "flip"): p_flip("p0", p0, f0["up_done"], CH),
                      ("p1", "flip"): p_flip("p1", p1, f1["up_done"], E1),
                      ("p0", "spread"): p0_spread, ("p1", "hidden"): p1_hidden,
                      ("p1", "route"): p1_route, ("p1", "spread"): p1_spread,
                      ("f0", "tail"): f0_tail, ("f1", "tail"): f1_tail}
            for k in ("g0", "g1"):
                pieces.update({(k, "flip"): gnn_flip(k), (k, "project"): gnn_project(k),
                               (k, "scores"): gnn_scores(k), (k, "softmax"): gnn_softmax(k)})
            for c in range(CH):
                pieces["f0", f"chunk{c}"] = f0_chunk(c)
            for e in range(E1):
                pieces["f1", f"up{e}"] = f1_up(e)
                pieces["f1", f"mid{e}"] = f1_mid(e)
                pieces["f1", f"down{e}"] = f1_down(e)
            run(act, pieces)

        @block.vector
        def _(dve):
            V = nc.vector
            links = [0]

            def link(ins):
                links[0] += 1
                ins.then_inc(setup_link, 1)
                dve.wait_ge(setup_link, links[0])

            dve.wait_ge(weights_in, LOADS)
            V.tensor_copy(ident16[:, :], ident[:, :])
            V.tensor_copy(pick16[:, :, :], pick_f32[:, :, :])
            dve.wait_ge(fills_done, 1)
            for name, full in bias_raw.items():
                width = full.shape[1]
                part, stacked = part_tmp[:, 0:width], bias16[name]
                for r in range(PARTS):
                    link(V.tensor_copy(part, full[:, :]))
                    link(V.tensor_copy(stacked[KR * r:KR * (r + 1), :], part[KR * r:KR * (r + 1), :]))
                    if r < PARTS - 1:
                        link(V.tensor_tensor(full[:, :], full[:, :], part, ALU.subtract))
            for n, name in enumerate(split_sources):
                dve.wait_ge(hi_split, n + 1)
                V.tensor_tensor(lo[name][:, :], raw[name][:, :], hi[name][:, :].bitcast(F32), ALU.subtract)
            dve.wait_ge(score_w_done, 2)
            for n, k in enumerate(("g0", "g1")):
                last = V.tensor_copy(gnn[k]["score_w"][:, :], value_bank[:, 2 * n:2 * n + 2])
            last.then_inc(setup_ready, 1)

            def stats(k, loaded=None):
                q = norm[k]

                def piece(g):
                    if k == "g0":
                        dve.wait_ge(x_in, 16 * (g + 1))
                    if k == "p0":
                        dve.wait_ge(gnn["g0"]["x_ready"], g + 1)
                    if k == "g1":
                        dve.wait_ge(f0["x_ready"], g + 1)
                    if k == "p1":
                        dve.wait_ge(gnn["g1"]["x_ready"], g + 1)
                    for b in range(GB):
                        last = V.bn_stats(q["stats"][:, b, :], q["src"][:, b, :])
                    last.then_inc(q["stats_done"], 1)
                    apart(dve)
                    dve.wait_ge(q["stats_done"], g + 1)
                    earlier(dve, q["normed_ready"], g)
                    for b in range(GB):
                        last = V.bn_aggr(q["mean_var"][:, b, :], q["stats"][:, b, :])
                    last.then_inc(q["var_ready"], 1)
                    if k == "g0":
                        dve.wait_ge(adj_in, 16 * (g + 1))
                        earlier(dve, gnn["g0"]["scores_done"], g)
                        earlier(dve, gnn["g1"]["mask_ready"], g)
                        V.tensor_scalar(gnn["g0"]["masked"][:, :], flat(adj_sb), 0.0, NEG_BIG, ALU.is_le,
                                        ALU.mult).then_inc(gnn["g0"]["mask_ready"], 1)
                return piece

            def gnn_project(k):
                q = gnn[k]

                def piece(g):
                    dve.wait_ge(q["src_dst_done"], g + 1)
                    earlier(dve, q["scores_ready"], g)
                    V.tensor_copy(q["src_dst"][:, :, :],
                                  score_bank[:, 0:2 * GB].rearrange("p (b s) -> p b s", s=2))\
                        .then_inc(q["src_dst_ready"], 1)
                    dve.wait_ge(q["src_dst_ready"], g + 1)
                    dst = q["src_dst"][:, :, 1]
                    V.tensor_copy(q["dst_parts"][:, :, 0], dst).then_inc(q["part1_ready"], 1)
                    dve.wait_ge(q["part1_ready"], g + 1)
                    V.tensor_tensor(q["rest1"][:, :], dst, q["dst_parts"][:, :, 0],
                                    ALU.subtract).then_inc(q["rest1_ready"], 1)
                    dve.wait_ge(q["rest1_ready"], g + 1)
                    V.tensor_copy(q["dst_parts"][:, :, 1], q["rest1"][:, :]).then_inc(q["part2_ready"], 1)
                    dve.wait_ge(q["part2_ready"], g + 1)
                    V.tensor_tensor(q["rest2"][:, :], q["rest1"][:, :], q["dst_parts"][:, :, 1],
                                    ALU.subtract).then_inc(q["rest2_ready"], 1)
                    dve.wait_ge(q["rest2_ready"], g + 1)
                    V.tensor_copy(q["dst_parts"][:, :, 2], q["rest2"][:, :]).then_inc(q["dst_parts_ready"], 1)
                return piece

            def gnn_row(k):
                q = gnn[k]

                def piece(g):
                    dve.wait_ge(q["rows_flipped"], g + 1)
                    V.tensor_copy(q["dst_rows"][:, :], flip16[0:KR, 0:T]).then_inc(q["rows_ready"], 1)
                return piece

            def gnn_scores(k):
                q = gnn[k]

                def piece(g):
                    dve.wait_ge(q["scores_ready"], g + 1)
                    V.tensor_reduce(q["neg_max"][:, :], q["scores"][:, :, :], AX_X, ALU.max, negate=True)\
                        .then_inc(q["neg_max_ready"], 1)
                    V.scalar_tensor_tensor(flat(q["leaky"]), flat(q["scores"]), SLOPE, flat(q["scores"]),
                                           ALU.mult, ALU.max).then_inc(q["leaky_ready"], 1)
                    dve.wait_ge(q["neg_max_ready"], g + 1)
                    V.scalar_tensor_tensor(q["neg_leaky_max"][:, :], q["neg_max"][:, :], SLOPE, q["neg_max"][:, :],
                                           ALU.mult, ALU.min).then_inc(q["neg_leaky_max_ready"], 1)
                return piece

            def gnn_flip_probs(k):
                q = gnn[k]

                def piece(g):
                    dve.wait_ge(q["probs_ready"], g + 1)
                    if k == "g0":
                        earlier(dve, mixed_relu_ready, g)
                    V.reciprocal(q["row_rcp"][:, :], q["row_sum"][:, :]).then_inc(q["row_rcp_ready"], 1)
                    dve.wait_ge(q["probs_flipped"], g + 1)
                    earlier(dve, q["mixed"], g)
                    V.tensor_copy(q["probs_t"][:, :], flip_bank[:, :]).then_inc(q["probs_t_ready"], 1)
                return piece

            def g1_mix(g):
                q = gnn["g1"]
                dve.wait_ge(q["mixed"], g + 1)
                dve.wait_ge(x2_bias_ready, g + 1)
                dve.wait_ge(q["row_rcp_ready"], g + 1)
                earlier(dve, norm["p1"]["normed_ready"], g)
                earlier(dve, x3_held_ready, g)
                for b in range(GB):
                    last = V.scalar_tensor_tensor(x3[:, b, :], per_graph(value_bank, b),
                                                  q["row_rcp"][:, b:b + 1], x2_bias[:, b, :],
                                                  ALU.mult, ALU.add)
                last.then_inc(q["x_ready"], 1)

            def p_flip(p):
                def piece(g):
                    dve.wait_ge(p["hi_ready"], g + 1)
                    V.tensor_tensor(p["lo"][:, :], flip_bank[:, :], p["hi"][:, :].bitcast(F32),
                                    ALU.subtract).then_inc(p["lo_ready"], 1)
                return piece

            def chain(p, g):
                n = [0]

                def step(ins):
                    n[0] += 1
                    ins.then_inc(p["link"], 1)
                    dve.wait_ge(p["link"], p["LINKS"] * g + n[0])
                return step, n

            def p0_route(g):
                step, n = chain(p0, g)
                dve.wait_ge(p0["logits_done"], g + 1)
                step(V.tensor_tensor(p0["logits"][:, :, :],
                                     score_bank[:, 0:GB * E0].rearrange("p (b e) -> p b e", e=E0),
                                     every_graph(rt0_b, E0), ALU.add))
                step(V.tensor_reduce(p0["top"][:, :], p0["logits"][:, :, :], AX_X, ALU.max))
                step(V.tensor_tensor(p0["at_top"][:, :, :], p0["logits"][:, :, :], wide(p0["top"], E0),
                                     ALU.is_equal))
                step(V.tensor_tensor(p0["ranked"][:, :, :], p0["at_top"][:, :, :], every_graph(rank0_sb, E0),
                                     ALU.mult))
                step(V.tensor_reduce(p0["first"][:, :], p0["ranked"][:, :, :], AX_X, ALU.max))
                assert n[0] == p0["LINKS"]
                earlier(dve, p0["spread_flipped"], g)
                V.tensor_tensor(
                    p0["onehot"][:, :, :, :],
                    p0["ranked"][:, :, :].unsqueeze(2).broadcast_to([P, GB, REP, E0]),
                    p0["first"][:, :].unsqueeze(2).unsqueeze(3).broadcast_to([P, GB, REP, E0]),
                    ALU.is_equal).then_inc(p0["onehot_ready"], 1)

            def p1_route(g):
                step, n = chain(p1, g)
                a, c = p1["t6"], p1["t1"]
                rank = every_graph(rank1_sb, E1)

                def full(name):
                    return a[name][:, :, :]

                def per_token(name):
                    return wide(c[name], E1)

                dve.wait_ge(p1["logits_done"], g + 1)
                step(V.tensor_tensor(full("logits"),
                                     score_bank[:, 0:GB * E1].rearrange("p (b e) -> p b e", e=E1),
                                     every_graph(rt2_b, E1), ALU.add))
                step(V.tensor_reduce(c["neg_max"][:, :], full("logits"), AX_X, ALU.max, negate=True))
                V.tensor_tensor(full("shifted"), full("logits"), per_token("neg_max"), ALU.add)\
                    .then_inc(p1["shifted_ready"], 1)
                dve.wait_ge(p1["exps_ready"], g + 1)
                step(V.tensor_reduce(c["sum"][:, :], full("exps"), AX_X, ALU.add))
                step(V.reciprocal(c["rcp"][:, :], c["sum"][:, :]))
                step(V.tensor_tensor(full("probs"), full("exps"), per_token("rcp"), ALU.mult))
                step(V.tensor_reduce(c["top"][:, :], full("probs"), AX_X, ALU.max))
                step(V.tensor_tensor(full("at_top"), full("probs"), per_token("top"), ALU.is_equal))
                step(V.tensor_tensor(full("ranked"), full("at_top"), rank, ALU.mult))
                step(V.tensor_reduce(c["rank_top"][:, :], full("ranked"), AX_X, ALU.max))
                step(V.tensor_tensor(full("first"), full("ranked"), per_token("rank_top"), ALU.is_equal))
                step(V.scalar_tensor_tensor(full("others"), full("first"), -4.0, full("probs"), ALU.mult,
                                            ALU.add))
                step(V.tensor_reduce(c["next"][:, :], full("others"), AX_X, ALU.max))
                V.tensor_tensor(c["gap"][:, :], c["next"][:, :], c["top"][:, :], ALU.subtract)\
                    .then_inc(p1["gap_ready"], 1)
                step(V.tensor_tensor(full("at_second"), full("others"), per_token("next"), ALU.is_equal))
                step(V.tensor_tensor(full("ranked2"), full("at_second"), rank, ALU.mult))
                step(V.tensor_reduce(c["rank_next"][:, :], full("ranked2"), AX_X, ALU.max))
                step(V.tensor_tensor(full("second"), full("ranked2"), per_token("rank_next"),
                                     ALU.is_equal))
                dve.wait_ge(p1["exp_gap_ready"], g + 1)
                step(V.tensor_scalar(c["gap_sum"][:, :], c["exp_gap"][:, :], 1.0, None, ALU.add))
                step(V.reciprocal(c["weight1"][:, :], c["gap_sum"][:, :]))
                step(V.tensor_tensor(c["weight2"][:, :], c["exp_gap"][:, :], c["weight1"][:, :],
                                     ALU.mult))
                step(V.tensor_tensor(full("gate1"), full("first"), per_token("weight1"), ALU.mult))
                step(V.tensor_tensor(full("gate2"), full("second"), per_token("weight2"), ALU.mult))
                step(V.tensor_tensor(full("gates"), full("gate1"), full("gate2"), ALU.add))
                earlier(dve, p1["spread_flipped"], g)
                v = p1["parts"][:, :, :, 0:E1 * PARTS].rearrange("p b r (e k) -> p b r e k", k=PARTS)

                def replicas(name):
                    return a[name][:, :, :].unsqueeze(2).broadcast_to([P, GB, REP, E1])

                step(V.tensor_copy(v[:, :, :, :, 0], replicas("gates")))
                step(V.tensor_tensor(full("rest1"), full("gates"), v[:, :, 0, :, 0], ALU.subtract))
                step(V.tensor_copy(v[:, :, :, :, 1], replicas("rest1")))
                step(V.tensor_tensor(full("rest2"), full("rest1"), v[:, :, 0, :, 1], ALU.subtract))
                assert n[0] == p1["LINKS"], n
                V.tensor_copy(v[:, :, :, :, 2], replicas("rest2")).then_inc(p1["parts_ready"], 1)

            def f0_chunk(c):
                def piece(g):
                    dve.wait_ge(f0["hi_ready"], nth(g, c, CH))
                    V.scalar_tensor_tensor(f0["lo"][c % 3][:, :], hid_bank[c % 3][:, :], 0.0,
                                           f0["hi"][c % 3][:, :].bitcast(F32), ALU.max,
                                           ALU.subtract).then_inc(f0["lo_ready"], 1)
                return piece

            def f0_tail(g):
                dve.wait_ge(f0["sum_flipped"], g + 1)
                dve.wait_ge(x1_held_ready, g + 1)
                earlier(dve, norm["g1"]["normed_ready"], g)
                earlier(dve, x2_bias_ready, g)
                V.tensor_tensor(flat(x2), flat(x1_held), gate_bank[:, :], ALU.add).then_inc(f0["x_ready"], 1)

            def f1_lo1(e, g):
                dve.wait_ge(f1["relu1_ready"], nth(g, e, E1))
                dve.wait_ge(f1["hi1_ready"], nth(g, e, E1))
                V.tensor_tensor(f1["lo1"][e % 2][:, :], f1["relu1"][e % 2][:, :],
                                f1["hi1"][e % 2][:, :].bitcast(F32), ALU.subtract)\
                    .then_inc(f1["lo1_ready"], 1)

            def f1_lo2(e, g):
                dve.wait_ge(f1["hi2_ready"], nth(g, e, E1))
                V.tensor_tensor(f1["lo2"][e % 2][:, :], f1["gated"][e % 2][:, :],
                                f1["hi2"][e % 2][:, :].bitcast(F32), ALU.subtract)\
                    .then_inc(f1["lo2_ready"], 1)

            def f1_up(e):
                def piece(g):
                    if e >= 2:
                        f1_lo2(e - 2, g)
                    f1_lo1(e, g)
                return piece

            def f1_mid(e):
                def piece(g):
                    dve.wait_ge(f1["relu2_ready"], nth(g, e, E1))
                    dve.wait_ge(f1["gate_done"], nth(g, e, E1))
                    V.tensor_tensor(f1["gated"][e % 2][:, :], f1["relu2"][e % 2][:, :], gate_bank[:, :],
                                    ALU.mult).then_inc(f1["gated_ready"], 1)
                return piece

            def f1_down(e):
                def piece(g):
                    if e >= E1 - 2:
                        f1_lo2(e, g)
                return piece

            def f1_tail(g):
                dve.wait_ge(f1["sum_flipped"], g + 1)
                dve.wait_ge(x3_held_ready, g + 1)
                if not isinstance(g, int) or g >= 1:
                    dve.wait_ge(x_out, 16 * g)
                V.tensor_tensor(flat(x4), flat(x3_held), gate_bank[:, :], ALU.add).then_inc(f1["x_ready"], 1)

            pieces = {("g1", "mix"): g1_mix, ("p0", "flip"): p_flip(p0), ("p1", "flip"): p_flip(p1),
                      ("p0", "route"): p0_route, ("p1", "route"): p1_route,
                      ("f0", "tail"): f0_tail, ("f1", "tail"): f1_tail}
            for k in norm:
                pieces[k, "norm"] = stats(k)
            for k in ("g0", "g1"):
                pieces.update({(k, "project"): gnn_project(k), (k, "row"): gnn_row(k),
                               (k, "scores"): gnn_scores(k), (k, "flip_probs"): gnn_flip_probs(k)})
            for c in range(CH):
                pieces["f0", f"chunk{c}"] = f0_chunk(c)
            for e in range(E1):
                pieces["f1", f"up{e}"] = f1_up(e)
                pieces["f1", f"mid{e}"] = f1_mid(e)
                pieces["f1", f"down{e}"] = f1_down(e)
            run(dve, pieces)

        @block.tensor
        def _(pe):
            M = nc.tensor.matmul

            def three(bank, w, cols, x_hi, x_lo, start, stop):
                M(bank[:, :], hi[w][:, cols], x_hi[:, :], start=start, stop=False)
                M(bank[:, :], hi[w][:, cols], x_lo[:, :], start=False, stop=False)
                return M(bank[:, :], lo[w][:, cols], x_hi[:, :], start=False, stop=stop)

            def columns(n):
                return slice(n * P, (n + 1) * P)

            pe.wait_ge(weights_in, LOADS)
            for n, k in enumerate(("g0", "g1")):
                M(value_bank[:, 2 * n:2 * n + 2], gnn[k]["w_turned"][:, :], gnn[k]["a"][:, :], start=True,
                  stop=True).then_inc(score_w_done, 1)
            pe.wait_ge(setup_ready, 1)
            pe.wait_ge(picked, PARTS)

            def flip(k, free):
                q = norm[k]

                def piece(g):
                    pe.wait_ge(q["normed_ready"], g + 1)
                    free(g)
                    for b in range(GB):
                        last = nc.tensor.transpose(per_graph(flip_bank, b), q["normed"][:, b, :], ident[:, :])
                    last.then_inc(q["flipped"], 1)
                return piece

            def g0_banks(g):
                earlier(pe, p0["spread_ready"], g)
                earlier(pe, p1["spread_ready"], g, 2)

            def g1_banks(g):
                pe.wait_ge(p0["spread_ready"], ahead(g, 1))
                earlier(pe, p1["spread_ready"], g)

            def no_wait(g):
                pass

            def gnn_project(k):
                q = gnn[k]

                def piece(g):
                    pe.wait_ge(q["normed_t_ready"], g + 1)
                    for b in range(GB):
                        last = M(score_bank[:, 2 * b:2 * b + 2], per_graph(q["normed_t"], b),
                                 q["score_w"][:, :], start=True, stop=True)
                    last.then_inc(q["src_dst_done"], 1)
                    for b in range(GB):
                        last = M(per_graph(value_bank, b), per_graph(q["normed_t"], b), q["w"][:, :],
                                 start=True, stop=True)
                    last.then_inc(q["values_done"], 1)
                return piece

            def gnn_row(k):
                q = gnn[k]

                def piece(g):
                    pe.wait_ge(q["dst_parts_ready"], g + 1)
                    for b in range(GB):
                        last = nc.tensor.transpose(flip16[0:KR, b * N:(b + 1) * N], q["dst_parts"][:, b, :],
                                                   ident16[:, :])
                    last.then_inc(q["rows_flipped"], 1)
                return piece

            def gnn_scores(k):
                q = gnn[k]

                def piece(g):
                    pe.wait_ge(q["mask_ready"], g + 1)
                    pe.wait_ge(q["rows_ready"], g + 1)
                    M(score_bank[:, :], ident16[:, :], q["masked"][:, :], start=True, stop=False)
                    M(score_bank[:, :], ones16[:, :], q["dst_rows"][:, :], start=False, stop=True)\
                        .then_inc(q["scores_done"], 1)
                return piece

            def gnn_flip_probs(k):
                q = gnn[k]

                def piece(g):
                    pe.wait_ge(q["probs_ready"], g + 1)
                    for b in range(GB):
                        last = nc.tensor.transpose(per_graph(flip_bank, b), q["probs"][:, b, :], ident[:, :])
                    last.then_inc(q["probs_flipped"], 1)
                return piece

            def gnn_mix(k):
                q = gnn[k]

                def piece(g):
                    pe.wait_ge(q["probs_t_ready"], g + 1)
                    pe.wait_ge(q["values_ready"], g + 1)
                    for b in range(GB):
                        last = M(per_graph(value_bank, b), per_graph(q["probs_t"], b), per_graph(q["values"], b),
                                 start=True, stop=True)
                    last.then_inc(q["mixed"], 1)
                return piece

            def p0_route(g):
                pe.wait_ge(p0["lo_ready"], g + 1)
                for b in range(GB):
                    out_cols = score_bank[:, b * E0:(b + 1) * E0]
                    M(out_cols, per_graph(p0["hi"], b).bitcast(F32), rt0[:, :], start=True, stop=False)
                    last = M(out_cols, per_graph(p0["lo"], b).bitcast(F32), rt0[:, :], start=False, stop=True)
                last.then_inc(p0["logits_done"], 1)

            def p0_spread(g):
                pe.wait_ge(p0["onehot_ready"], g + 1)
                for b in range(GB):
                    last = nc.tensor.transpose(flip16[:, b * N:(b + 1) * N],
                                               p0["onehot"][:, b, :, :].rearrange("p r e -> p (r e)"),
                                               ident16[:, :])
                last.then_inc(p0["spread_flipped"], 1)

            def p1_hidden(g):
                pe.wait_ge(p1["lo_ready"], g + 1)
                three(score_bank, "rt1", columns(0), p1["hi"], p1["lo"], True, True).then_inc(p1["hidden_done"], 1)

            def p1_route(g):
                pe.wait_ge(p1["hidden_ready"], g + 1)
                for b in range(GB):
                    last = M(score_bank[:, b * E1:(b + 1) * E1], per_graph(p1["hidden"], b), rt2[:, :],
                             start=True, stop=True)
                last.then_inc(p1["logits_done"], 1)

            def p1_spread(g):
                pe.wait_ge(p1["parts_ready"], g + 1)
                for b in range(GB):
                    last = nc.tensor.transpose(flip16[:, b * N:(b + 1) * N],
                                               p1["parts"][:, b, :, :].rearrange("p r k -> p (r k)"),
                                               ident16[:, :])
                last.then_inc(p1["spread_flipped"], 1)

            def f0_chunk(c):
                def piece(g):
                    if c < CH:
                        if c == 0:
                            pe.wait_ge(p0["lo_ready"], g + 1)
                            pe.wait_ge(p0["spread_ready"], g + 1)
                        if c >= 3:
                            pe.wait_ge(f0["lo_ready"], nth(g, c - 3, CH))
                        M(hid_bank[c % 3][:, :], bias16["b1_f0"][:, columns(c)], p0["spread"][:, :],
                          start=True, stop=False)
                        three(hid_bank[c % 3], "w1_f0", columns(c), p0["hi"], p0["lo"], False, True)\
                            .then_inc(f0["up_done"], 1)
                    d = c - 2
                    if d >= 0:
                        if d == 0:
                            M(out_bank[:, :], bias16["b2_f0"][:, :], p0["spread"][:, :], start=True,
                              stop=False)
                        pe.wait_ge(f0["lo_ready"], nth(g, d, CH))
                        three(out_bank, "w2_f0", columns(d), f0["hi"][d % 3], f0["lo"][d % 3], False,
                              d == CH - 1).then_inc(f0["down_done"], 1)
                return piece

            def tail(f):
                def piece(g):
                    pe.wait_ge(f["sum_ready"], g + 1)
                    if f is f0:
                        earlier(pe, f1["x_ready"], g, 2)
                    for b in range(GB):
                        last = nc.tensor.transpose(per_graph(gate_bank, b), per_graph(f["sum_t"], b),
                                                   ident[:, :])
                    last.then_inc(f["sum_flipped"], 1)
                return piece

            def f1_up(e):
                def piece(g):
                    if e == 0:
                        pe.wait_ge(p1["spread_ready"], g + 1)
                    three(hid_bank[max(0, 2 * e - 1) % 3], "w1_f1", columns(e), p1["hi"], p1["lo"], True, True)\
                        .then_inc(f1["up_done"], 1)
                return piece

            def f1_mid(e):
                def piece(g):
                    if e == 0:
                        pe.wait_ge(f0["x_ready"], ahead(g, 1))
                    else:
                        pe.wait_ge(f1["gated_ready"], nth(g, e - 1, E1))
                    M(gate_bank[:, :], pick16[:, e, :], p1["spread"][:, :], start=True, stop=True)\
                        .then_inc(f1["gate_done"], 1)
                    pe.wait_ge(f1["lo1_ready"], nth(g, e, E1))
                    three(hid_bank[(2 * e + 2) % 3], "w2_f1", columns(e), f1["hi1"][e % 2], f1["lo1"][e % 2],
                          True, True).then_inc(f1["mid_done"], 1)
                return piece

            def f1_down(e):
                def piece(g):
                    if e == 0:
                        M(out_bank[:, :], bias16["b3_f1"][:, :], p1["spread"][:, :], start=True, stop=False)
                    pe.wait_ge(f1["lo2_ready"], nth(g, e, E1))
                    three(out_bank, "w3_f1", columns(e), f1["hi2"][e % 2], f1["lo2"][e % 2], False,
                          e == E1 - 1).then_inc(f1["down_done"], 1)
                return piece

            pieces = {("g0", "flip"): flip("g0", g0_banks), ("g1", "flip"): flip("g1", g1_banks),
                      ("p0", "flip"): flip("p0", no_wait), ("p1", "flip"): flip("p1", no_wait),
                      ("p0", "route"): p0_route, ("p0", "spread"): p0_spread,
                      ("p1", "hidden"): p1_hidden, ("p1", "route"): p1_route,
                      ("p1", "spread"): p1_spread, ("f0", "tail"): tail(f0), ("f1", "tail"): tail(f1)}
            for k in ("g0", "g1"):
                pieces.update({(k, "project"): gnn_project(k), (k, "row"): gnn_row(k),
                               (k, "scores"): gnn_scores(k), (k, "flip_probs"): gnn_flip_probs(k),
                               (k, "mix"): gnn_mix(k)})
            for c in range(CH + 2):
                pieces["f0", f"chunk{c}"] = f0_chunk(c)
            for e in range(E1):
                pieces["f1", f"up{e}"] = f1_up(e)
                pieces["f1", f"mid{e}"] = f1_mid(e)
                pieces["f1", f"down{e}"] = f1_down(e)
            run(pe, pieces)


def kernel(x, adj, L0_gnn_W, L0_gnn_a, L0_ffn_router_w, L0_ffn_router_b, L0_ffn_W1, L0_ffn_b1, L0_ffn_W2,
           L0_ffn_b2, L1_gnn_W, L1_gnn_a, L1_gnn_bias, L1_ffn_router_w1, L1_ffn_router_b1,
           L1_ffn_router_w2, L1_ffn_router_b2, L1_ffn_expert_w1, L1_ffn_expert_b1, L1_ffn_expert_w2,
           L1_ffn_expert_b2, L1_ffn_expert_w3, L1_ffn_expert_b3):
    import numpy as np
    import concourse.bacc as bacc
    from concourse import mybir as mb
    from concourse.bass_utils import run_bass_kernel_spmd

    D = x.shape[2]
    E0, E1, R1 = L0_ffn_router_w.shape[0], L1_ffn_router_w2.shape[1], L1_ffn_router_w1.shape[1]
    REP, KR, PARTS = 4, 32, 3

    def widened(a, shape):
        out = np.zeros(shape, a.dtype)
        out[tuple(slice(0, n) for n in a.shape)] = a
        return out

    def experts_inside(w):
        return w.transpose(1, 0, 2).reshape(w.shape[1], -1)

    pick = np.zeros((128, E1, 128), np.float32)
    for e in range(E1):
        pick[e * PARTS:(e + 1) * PARTS, e, :] = 1.0
    ins = {
        "x": x, "adj": adj,
        "g0_w": L0_gnn_W, "g0_w_turned": L0_gnn_W.T, "g0_a": L0_gnn_a.reshape(2, D).T,
        "g1_w": L1_gnn_W.T, "g1_w_turned": L1_gnn_W, "g1_a": L1_gnn_a.T, "g1_bias": L1_gnn_bias,
        "f0_router": L0_ffn_router_w.T, "f0_router_b": L0_ffn_router_b,
        "f0_w1": experts_inside(L0_ffn_W1), "f0_b1": L0_ffn_b1.reshape(-1),
        "f0_w2": L0_ffn_W2.reshape(-1, D), "f0_b2": np.tile(L0_ffn_b2, (REP, 1)),
        "f1_router1": widened(L1_ffn_router_w1, (D, 128)),
        "f1_router1_b": widened(L1_ffn_router_b1.reshape(R1, 1), (128, 1)),
        "f1_router2": widened(L1_ffn_router_w2, (128, E1)), "f1_router2_b": L1_ffn_router_b2,
        "f1_w1": experts_inside(L1_ffn_expert_w1), "f1_b1": L1_ffn_expert_b1.T,
        "f1_w2": experts_inside(L1_ffn_expert_w2), "f1_b2": L1_ffn_expert_b2.T,
        "f1_w3": experts_inside(L1_ffn_expert_w3),
        "f1_b3": np.tile(widened(np.repeat(L1_ffn_expert_b3, PARTS, axis=0), (KR, D)), (REP, 1)),
        "eye": np.eye(128, dtype=np.float32),
        "rank0": np.tile(np.arange(E0, 0, -1, dtype=np.float32), (128, 1)),
        "rank1": np.tile(np.arange(E1, 0, -1, dtype=np.float32), (128, 1)),
        "gate_pick": pick,
    }
    nc = bacc.Bacc("TRN2", target_bir_lowering=False, num_devices=1)
    arrays, args = {}, []
    for name, a in ins.items():
        arrays[f"in_{name}"] = np.ascontiguousarray(a)
        args.append(nc.dram_tensor(f"in_{name}", a.shape, mb.dt.from_np(a.dtype), kind="ExternalInput").ap())
    args.append(nc.dram_tensor("out_x", x.shape, mb.dt.from_np(x.dtype), kind="ExternalOutput").ap())
    four_layer_kernel(nc, *args)
    return run_bass_kernel_spmd(nc, [arrays], core_ids=[0]).results[0]["out_x"]
```

```python
from contextlib import ExitStack

import concourse.bass as bass
from concourse import mybir

F32 = mybir.dt.float32
F32R = mybir.dt.float32r
BF16 = mybir.dt.bfloat16
I32 = mybir.dt.int32
ALU = mybir.AluOpType
ACT = mybir.ActivationFunctionType
AX_X = mybir.AxisListType.X

NEG_BIG = -9000000000000000.0
SLOPE = 0.2
EPS = 1e-5
UNSELECTED = -1e30

PE_ORDER = [
    (2, "f0_down5"), (4, "f1_up0"), (2, "f0_down6"), (2, "f0_down7"), (3, "g1_flip_probs"),
    (4, "f1_up1"), (2, "t0_turn"), (1, "p0_flip"), (3, "g1_mix"), (4, "f1_mid0"), (4, "f1_up2"),
    (1, "p0_route"), (0, "g0_flip"), (4, "f1_mid1"), (4, "f1_up3"), (0, "g0_project"), (4, "f1_mid2"),
    (4, "f1_up4"), (4, "f1_down0"), (0, "g0_row"), (4, "f1_mid3"), (4, "f1_up5"), (1, "p0_turn"),
    (0, "g0_score"), (4, "f1_down1"), (4, "f1_mid4"), (1, "f0_up0"), (3, "p1_flip"), (4, "f1_down2"),
    (1, "f0_up1"), (4, "f1_down3"), (4, "f1_mid5"), (3, "p1_hide"), (0, "g0_flip_probs"),
    (1, "f0_up2"), (3, "p1_route"), (0, "g0_mix"), (1, "f0_up3"), (2, "g1_flip"), (1, "f0_up4"),
    (4, "f1_down4"), (4, "f1_down5"), (2, "g1_project"), (4, "f1_turn"), (1, "f0_down0"),
    (1, "f0_down1"), (1, "f0_down2"), (2, "g1_row"), (1, "f0_up5"), (1, "f0_down3"), (2, "g1_score"),
    (1, "f0_up6"), (1, "f0_up7"), (3, "p1_turn"), (1, "f0_down4")]
ACT_ORDER = [
    (1, "p0_hi"), (1, "p0_full"), (4, "f1_relu1_1"), (4, "f1_relu2_0"), (4, "f1_relu1_2"),
    (4, "f1_hi1_2"), (4, "f1_hi2_0"), (0, "g0_normed_t"), (4, "f1_relu2_1"), (4, "f1_relu1_3"),
    (4, "f1_hi1_3"), (4, "f1_hi2_1"), (4, "f1_relu2_2"), (4, "f1_relu1_4"), (4, "f1_hi1_4"),
    (0, "g0_values"), (4, "f1_relu2_3"), (4, "f1_hi2_2"), (4, "f1_relu1_5"), (1, "p0_spread"),
    (4, "f1_hi2_3"), (4, "f1_hi1_5"), (4, "f1_relu2_4"), (3, "p1_hi"), (3, "p1_full"), (1, "f0_hi0"),
    (0, "g0_softmax"), (4, "f1_relu2_5"), (3, "p1_hidden"), (1, "f0_hi1"), (0, "g0_probs_t"),
    (4, "f1_hi2_4"), (4, "f1_hi2_5"), (1, "f0_hi2"), (0, "g0_relu"), (3, "p1_exps"),
    (2, "g1_normed_t"), (3, "p1_exp_next"), (4, "f1_sum"), (3, "p1_exp_gap"), (2, "g1_values"),
    (1, "f0_hi3"), (1, "f0_hi4"), (1, "f0_hi5"), (1, "f0_hi6"), (3, "p1_spread"), (1, "f0_hi7"),
    (2, "g1_softmax"), (3, "f1_relu1_0"), (1, "t0_sum"), (2, "g1_probs_t"), (3, "f1_hi1_0"),
    (3, "f1_hi1_1")]
DVE_ORDER = [
    (1, "g0_scores"), (1, "g0_leaky"), (5, "f1_gated_4"), (5, "f1_lo1_5"), (3, "g1_stats"),
    (3, "g1_aggregate"), (3, "g1_mask"), (2, "f0_lo0"), (1, "g0_row_rcp"), (5, "f1_gated_5"),
    (3, "g1_apply"), (2, "f0_lo1"), (4, "p1_route0"), (4, "p1_route1"), (4, "p1_route2"),
    (4, "p1_route3"), (4, "p1_route4"), (4, "p1_route5"), (4, "p1_route6"), (4, "p1_route7"),
    (4, "p1_route8"), (2, "f0_lo2"), (4, "p1_route9"), (4, "p1_route10"), (4, "p1_route11"),
    (4, "p1_route12"), (4, "p1_route13"), (4, "p1_route14"), (3, "g1_src_dst"), (1, "p0_stats"),
    (4, "p1_route15"), (4, "p1_route16"), (4, "p1_route17"), (4, "p1_route18"), (4, "p1_route19"),
    (2, "f0_lo3"), (4, "p1_route20"), (3, "g1_rows"), (2, "f0_lo4"), (1, "p0_aggregate"),
    (3, "g1_scores"), (2, "f0_lo5"), (3, "g1_leaky"), (2, "f0_lo6"), (2, "f0_lo7"), (5, "f1_add"),
    (0, "g0_stats"), (0, "g0_aggregate"), (0, "g0_mask"), (3, "g1_row_rcp"), (2, "t0_add"),
    (4, "f1_lo1_0"), (3, "g1_add"), (4, "f1_lo1_1"), (4, "f1_gated_0"), (3, "p1_stats"),
    (1, "p0_route0"), (4, "f1_lo1_2"), (1, "p0_route1"), (4, "f1_gated_1"), (1, "p0_route2"),
    (0, "g0_src_dst"), (1, "p0_route3"), (3, "p1_aggregate"), (1, "p0_route4"), (4, "f1_lo1_3"),
    (4, "f1_gated_2"), (1, "p0_route5"), (0, "g0_rows"), (4, "f1_lo1_4"), (4, "f1_gated_3"),
    (3, "p1_apply")]
POOL_ORDER = [
    (3, "g1_parts"), (4, "p1_parts"), (1, "p0_rstd"), (1, "p0_apply"), (4, "f1_hold"), (0, "g0_rstd"),
    (0, "g0_apply"), (1, "p0_lo"), (4, "f1_lo2_0"), (0, "g0_parts"), (4, "f1_lo2_1"), (3, "p1_rstd"),
    (1, "f0_hold"), (4, "f1_lo2_2"), (4, "f1_lo2_3"), (3, "p1_lo"), (2, "g1_rstd"), (4, "f1_lo2_4"),
    (4, "f1_lo2_5"), (2, "g1_bias"), (0, "g0_add")]
SP_ORDER = [
    (0, "x_load"), (0, "g0_adj"), (5, "x_store"), (1, "g1_adj")]
DEPTH = max(lag for order in (PE_ORDER, ACT_ORDER, DVE_ORDER, POOL_ORDER, SP_ORDER) for lag, _ in order)
F1_BEHIND = 3


def four_layer_kernel(nc, x, adj, g0_w, g0_w_turned, g0_a, g1_w, g1_w_turned, g1_a, g1_bias,
                      f0_router, f0_router_b, f0_w1, f0_b1, f0_w2, f0_b2,
                      f1_router1, f1_router1_b, f1_router2, f1_router2_b,
                      f1_w1, f1_b1, f1_w2, f1_b2, f1_w3, f1_b3,
                      eye, rank0, rank1, gate_pick, out):
    B, N, D = x.shape
    P = 128
    assert N == P and D == P
    GB = 4
    T = GB * N
    GROUPS = B // GB
    E0 = f0_router.shape[1]
    CH = f0_w1.shape[1] // P
    R1 = f1_router1.shape[1]
    E1 = f1_router2.shape[1]
    KR = 32
    REP = P // KR
    PARTS = 3

    ctx = ExitStack()
    with ctx:
        def sb(name, shape, dt=F32):
            return ctx.enter_context(nc.sbuf_tensor(name, shape, dt))

        def sem(name):
            return ctx.enter_context(nc.semaphore(name))

        hid_bank = [ctx.enter_context(nc.psum_tensor(f"hid_bank{i}", [P, T], F32)) for i in range(3)]
        out_bank = ctx.enter_context(nc.psum_tensor("out_bank", [P, T], F32))
        gate_bank = ctx.enter_context(nc.psum_tensor("gate_bank", [P, T], F32))
        flip_bank = ctx.enter_context(nc.psum_tensor("flip_bank", [P, T], F32))
        score_bank = ctx.enter_context(nc.psum_tensor("score_bank", [P, T], F32))
        value_bank = ctx.enter_context(nc.psum_tensor("value_bank", [P, T], F32))
        WIDE = T // (D + 2)
        value_cols = value_bank[:, 0:WIDE * (D + 2)].rearrange("p (b c) -> p b c", c=D + 2)
        flip16 = flip_bank[:, :].bitcast(BF16)
        f0_bank = [hid_bank[(2 - c) % 3] for c in range(CH)]
        f1_up_bank = [hid_bank[max(0, 2 * e - 1) % 3] for e in range(E1)]
        f1_mid_bank = [hid_bank[(2 * e + 2) % 3] for e in range(E1)]

        ident = sb("ident", [P, P])
        ident16 = sb("ident16", [P, P], BF16)
        ones16 = sb("ones16", [KR, P], BF16)
        minus_half = sb("minus_half", [P, GB])
        eps_sb = sb("eps_sb", [P, GB])
        one_sb = sb("one_sb", [P, 1])
        rank0_sb = sb("rank0_sb", [P, E0])
        rank1_sb = sb("rank1_sb", [P, E1])
        pick_f32 = sb("pick_f32", [P, E1, P])
        pick16 = sb("pick16", [P, E1, P], BF16)
        bias_g1 = sb("bias_g1", [P, D])
        rt0 = sb("rt0", [P, E0])
        rt0_b = sb("rt0_b", [P, E0])
        rt1_b = sb("rt1_b", [P, 1])
        rt2 = sb("rt2", [P, E1])
        rt2_b = sb("rt2_b", [P, E1])
        b1_f1 = sb("b1_f1", [P, E1])
        b2_f1 = sb("b2_f1", [P, E1])
        split_sources = {
            "w1_f0": (CH * P, f0_w1), "w2_f0": (CH * P, f0_w2.rearrange("(c p) d -> p c d", p=P)),
            "rt1": (R1, f1_router1), "w1_f1": (E1 * P, f1_w1), "w2_f1": (E1 * P, f1_w2),
            "w3_f1": (E1 * P, f1_w3)}
        raw, hi, lo = {}, {}, {}
        for name, (cols, _) in split_sources.items():
            raw[name] = sb(f"{name}_raw", [P, cols])
            hi[name] = sb(f"{name}_hi", [P, cols], F32R)
            lo[name] = sb(f"{name}_lo", [P, cols], F32R)
        bias_raw = {"b1_f0": sb("b1_f0_raw", [P, CH * P]), "b2_f0": sb("b2_f0_raw", [P, D]),
                    "b3_f1": sb("b3_f1_raw", [P, D])}
        bias16 = {"b1_f0": sb("b1_f0_16", [P, CH * P], BF16), "b2_f0": sb("b2_f0_16", [P, D], BF16),
                  "b3_f1": sb("b3_f1_16", [P, D], BF16)}
        part_tmp = {name: sb(f"{name}_part", list(full.shape), BF16) for name, full in bias_raw.items()}

        x0 = sb("x0", [P, GB, D])
        x1 = sb("x1", [P, GB, D])
        x1_held = sb("x1_held", [P, GB, D])
        x2 = sb("x2", [P, GB, D])
        x2_bias = sb("x2_bias", [P, GB, D])
        x3 = sb("x3", [P, GB, D])
        x3_held = sb("x3_held", [P, GB, D])
        x4 = sb("x4", [P, GB, D])


        norm = {}
        for k, src in (("g0", x0), ("p0", x1), ("g1", x2), ("p1", x3)):
            norm[k] = dict(
                src=src, stats=sb(f"{k}_stats", [P, GB, 6]), mean_var=sb(f"{k}_mean_var", [P, GB, 2]),
                var_eps=sb(f"{k}_var_eps", [P, GB]), rstd=sb(f"{k}_rstd", [P, GB]),
                normed=sb(f"{k}_normed", [P, GB, D]), centred=sb(f"{k}_centred", [P, GB, D]),
                **{s: sem(f"{k}_{s}") for s in ("stats_done", "var_ready", "eps_added", "rstd_ready", "centred_ready",
                                                "normed_ready", "flipped")})

        gnn = {}
        for k, w, w_turned, a in (("g0", g0_w, g0_w_turned, g0_a), ("g1", g1_w, g1_w_turned, g1_a)):
            gnn[k] = dict(
                w_dram=w, w_turned_dram=w_turned, a_dram=a,
                w=sb(f"{k}_w", [P, D + 2]),
                w_turned=sb(f"{k}_w_turned", [P, D]),
                a=sb(f"{k}_a", [P, 2]),
                adj=sb(f"{k}_adj", [P, GB, N], I32), adj_in=sem(f"{k}_adj_in"),
                masked=sb(f"{k}_masked", [P, T], BF16),
                normed_t=sb(f"{k}_normed_t", [P, T]),
                values=sb(f"{k}_values", [P, T]),
                src_dst=sb(f"{k}_src_dst", [P, GB, 2]),
                rest1=sb(f"{k}_rest1", [P, GB]),
                dst_parts=sb(f"{k}_dst_parts", [P, GB, KR], BF16),
                dst_rows=sb(f"{k}_dst_rows", [KR, T], BF16),
                scores=sb(f"{k}_scores", [P, GB, N]), leaky=sb(f"{k}_leaky", [P, GB, N]),
                neg_max=sb(f"{k}_neg_max", [P, GB]), neg_leaky_max=sb(f"{k}_neg_leaky_max", [P, GB]),
                probs=sb(f"{k}_probs", [P, GB, N]), row_sum=sb(f"{k}_row_sum", [P, GB]),
                row_rcp=sb(f"{k}_row_rcp", [P, GB]), probs_t=sb(f"{k}_probs_t", [P, T]),
                **{s: sem(f"{k}_{s}") for s in (
                    "mask_ready", "normed_t_ready", "values_done", "src_dst_ready",
                    "part1_ready", "rest1_ready", "part2_ready", "dst_parts_ready",
                    "rows_flipped", "rows_ready", "scores_done", "values_ready", "scores_ready",
                    "neg_max_ready", "neg_leaky_max_ready", "leaky_ready", "probs_ready",
                    "row_rcp_ready", "probs_flipped", "probs_t_ready", "mixed", "x_ready")})
        mixed_relu = sb("mixed_relu", [P, GB, D])
        mixed_relu_ready = sem("mixed_relu_ready")
        x2_bias_ready = sem("x2_bias_ready")
        x1_held_ready = sem("x1_held_ready")
        x3_held_ready = sem("x3_held_ready")

        p0 = dict(
            full=sb("p0_full", [P, T]), hi=sb("p0_hi", [P, T], F32R), lo=sb("p0_lo", [P, T], F32R),
            logits=sb("p0_logits", [P, GB, E0]), top=sb("p0_top", [P, GB]),
            at_top=sb("p0_at_top", [P, GB, E0]), ranked=sb("p0_ranked", [P, GB, E0]),
            first=sb("p0_first", [P, GB]), onehot=sb("p0_onehot", [P, GB, REP, E0], BF16),
            spread=sb("p0_spread", [P, T], BF16),
            link=sem("p0_link"), LINKS=5,
            **{s: sem(f"p0_{s}") for s in ("full_ready", "hi_ready", "lo_ready", "logits_done", "onehot_ready",
                                           "spread_flipped", "spread_ready")})
        p1 = dict(
            full=sb("p1_full", [P, T]), hi=sb("p1_hi", [P, T], F32R), lo=sb("p1_lo", [P, T], F32R),
            hidden=sb("p1_hidden", [P, T]),
            t6={s: sb(f"p1_{s}", [P, GB, E1]) for s in (
                "logits", "shifted", "exps", "ranked", "first", "others", "at_second", "ranked2", "second",
                "gate1", "gate2", "gates", "rest1")},
            t1={s: sb(f"p1_{s}", [P, GB]) for s in (
                "neg_max", "sum", "rcp", "rank_top", "next", "rank_next", "exp_next", "gap", "exp_gap",
                "gap_sum", "weight1", "weight2")},
            parts=sb("p1_parts", [P, GB, REP, KR], BF16),
            spread=sb("p1_spread", [P, T], BF16),
            link=sem("p1_link"), LINKS=21,
            **{s: sem(f"p1_{s}") for s in (
                "full_ready", "hi_ready", "lo_ready", "hidden_done", "hidden_ready", "logits_done", "exps_ready",
                "exp_next_ready", "exp_gap_ready", "part_link", "parts_ready", "spread_flipped",
                "spread_ready")})

        f0 = dict(
            hi=[sb(f"f0_hi{i}", [P, T], F32R) for i in range(3)],
            lo=[sb(f"f0_lo{i}", [P, T], F32R) for i in range(3)], sum_t=sb("f0_sum_t", [P, T]),
            **{s: sem(f"f0_{s}") for s in (
                "up_done", "hi_ready", "lo_ready", "down_done", "sum_ready", "sum_flipped", "x_ready")})
        f1 = dict(
            relu1=[sb(f"f1_relu1_{i}", [P, T]) for i in range(2)],
            hi1=[sb(f"f1_hi1_{i}", [P, T], F32R) for i in range(2)],
            lo1=[sb(f"f1_lo1_{i}", [P, T], F32R) for i in range(2)],
            relu2=[sb(f"f1_relu2_{i}", [P, T]) for i in range(2)],
            gated=[sb(f"f1_gated_{i}", [P, T]) for i in range(2)],
            hi2=[sb(f"f1_hi2_{i}", [P, T], F32R) for i in range(2)],
            lo2=[sb(f"f1_lo2_{i}", [P, T], F32R) for i in range(2)],
            sum_t=sb("f1_sum_t", [P, T]),
            **{s: sem(f"f1_{s}") for s in (
                "up_done", "relu1_ready", "hi1_ready", "lo1_ready", "gate_done", "mid_done",
                "relu2_ready", "gated_ready", "hi2_ready", "lo2_ready", "down_done",
                "sum_ready", "sum_flipped", "x_ready")})

        first_in = sem("first_in")
        weights_in = sem("weights_in")
        x_in = sem("x_in")
        x_out = sem("x_out")
        fills_done = sem("fills_done")
        hi_split = sem("hi_split")
        part_done = {name: sem(f"{name}_part_done") for name in bias_raw}
        BIAS_STEPS = 3 * PARTS - 1
        lo_split = sem("lo_split")
        picked = sem("picked")
        score_w_done = sem("score_w_done")
        setup_ready = sem("setup_ready")

        plain_loads = [
            (rank0_sb, rank0), (rank1_sb, rank1), (pick_f32, gate_pick),
            (bias_g1, g1_bias.partition_broadcast(P)), (rt0, f0_router),
            (rt0_b, f0_router_b.partition_broadcast(P)), (rt1_b, f1_router1_b), (rt2, f1_router2),
            (rt2_b, f1_router2_b.partition_broadcast(P)), (b1_f1, f1_b1), (b2_f1, f1_b2),
            (bias_raw["b1_f0"], f0_b1.partition_broadcast(P)), (bias_raw["b2_f0"], f0_b2),
            (bias_raw["b3_f1"], f1_b3)]
        first_loads = [(ident[:, :], eye)]
        for k in ("g0", "g1"):
            q = gnn[k]
            first_loads += [(q["w_turned"][:, :], q["w_turned_dram"]), (q["a"][:, :], q["a_dram"]),
                            (q["w"][:, 0:D], q["w_dram"])]
        FIRST_LOADS = 16 * len(first_loads)
        LOADS = 16 * (len(plain_loads) + len(split_sources))
        NSPLIT = len(split_sources)

        x_groups = x.rearrange("(g b) n d -> g n b d", b=GB)
        adj_groups = adj.rearrange("(g b) n m -> g n b m", b=GB)
        out_groups = out.rearrange("(g b) n d -> g n b d", b=GB)

        def per_graph(tile, b, width=N):
            return tile[:, b * width:(b + 1) * width]

        def flat(tile):
            return tile[:, :, :].rearrange("p b n -> p (b n)")

        def wide(column, width):
            return column[:, :].unsqueeze(2).broadcast_to([P, GB, width])

        def every_graph(row, width):
            return row[:, :].unsqueeze(1).broadcast_to([P, GB, width])

        def nth(g, i, n):
            return g * n + (i + 1)

        def earlier(eng, signal, g, back=1, i=0, n=1):
            if not isinstance(g, int) or g >= back:
                eng.wait_ge(signal, nth(g - back, i, n))

        def reached(eng, signal, g, by, i=0, n=1):
            if isinstance(g, int):
                if g + by >= 0:
                    eng.wait_ge(signal, nth(min(g + by, GROUPS - 1), i if g + by < GROUPS else n - 1, n))
            else:
                eng.wait_ge(signal, nth(g + by, i, n))

        def apart(eng):
            eng.wait_ge(fills_done, 1)

        def run(eng, order, pieces, setup=(), after=0):
            assert sorted(name for _, name in order) == sorted(pieces)

            def step(t, inside):
                for lag, name in order:
                    if inside or 0 <= t - lag < GROUPS:
                        pieces[name](t - lag)
                        done[0] += 1
                        if 0 < done[0] - after <= len(setup):
                            setup[done[0] - after - 1]()
            done = [0]
            for t in range(DEPTH + 1):
                step(t, False)
            assert done[0] >= after + len(setup)
            with eng.Fori(DEPTH + 1, GROUPS) as t:
                step(t, True)
            for t in range(GROUPS, GROUPS + DEPTH):
                step(t, False)

        block = ctx.enter_context(nc.Block())

        @block.sync
        def _(sp):
            def x_load(g):
                earlier(sp, gnn["g0"]["x_ready"], g)
                sp.dma_start(x0[:, :, :], x_groups[g]).then_inc(x_in, 16)

            def adj_load(k):
                q = gnn[k]

                def piece(g):
                    earlier(sp, q["mask_ready"], g)
                    sp.dma_start(q["adj"][:, :, :], adj_groups[g]).then_inc(q["adj_in"], 16)
                return piece

            def x_store(g):
                sp.wait_ge(f1["x_ready"], g + 1)
                sp.dma_start(out_groups[g], x4[:, :, :]).then_inc(x_out, 16)

            pieces = {"x_load": x_load, "g0_adj": adj_load("g0"), "g1_adj": adj_load("g1"),
                      "x_store": x_store}
            def load_weights():
                for tile, src in plain_loads:
                    dst = tile[:, :, :] if len(tile.shape) == 3 else tile[:, :]
                    sp.dma_start(dst, src).then_inc(weights_in, 16)
                for name, (_, src) in split_sources.items():
                    dst = raw[name][:, :]
                    if len(src.shape) == 3:
                        dst = dst.rearrange("p (c d) -> p c d", d=src.shape[2])
                    sp.dma_start(dst, src).then_inc(weights_in, 16)

            run(sp, SP_ORDER, pieces, [load_weights], after=1)
            sp.wait_ge(x_out, 16 * GROUPS)

        @block.gpsimd
        def _(pool):
            nc.gpsimd.memset(ones16[:, :], 1.0)
            nc.gpsimd.memset(minus_half[:, :], -0.5)
            nc.gpsimd.memset(eps_sb[:, :], EPS)
            nc.gpsimd.memset(one_sb[:, :], 1.0)
            nc.gpsimd.memset(p1["parts"][:, :, :, :], 0.0)
            for k in ("g0", "g1"):
                nc.gpsimd.memset(gnn[k]["dst_parts"][:, :, :], 0.0)
            nc.gpsimd.memset(bias16["b2_f0"][:, :], 0.0)
            nc.gpsimd.memset(bias16["b3_f1"][:, :], 0.0)
            nc.gpsimd.memset(bias16["b1_f0"][:, :], 0.0).then_inc(fills_done, 1)
            pool.wait_ge(fills_done, 1)

            def pick_expert():
                pool.wait_ge(part_done["b1_f0"], BIAS_STEPS)
                for r in range(PARTS):
                    v = bias16["b1_f0"][KR * r:KR * (r + 1), :].rearrange("p (e h) -> p e h", e=E0)
                    nc.gpsimd.affine_select(out=v, in_=v, compare_op=ALU.is_equal,
                                            fill=UNSELECTED if r == 0 else 0.0, base=0,
                                            pattern=[[-1, E0], [0, CH * P // E0]],
                                            channel_multiplier=1).then_inc(picked, 1)
                    pool.wait_ge(picked, r + 1)

            def rstd(k):
                q = norm[k]

                def piece(g):
                    pool.wait_ge(q["var_ready"], g + 1)
                    nc.gpsimd.tensor_tensor(q["var_eps"][:, :], q["mean_var"][:, :, 1], eps_sb[:, :],
                                            ALU.add).then_inc(q["eps_added"], 1)
                    pool.wait_ge(q["eps_added"], g + 1)
                    earlier(pool, q["normed_ready"], g)
                    nc.gpsimd.tensor_tensor(q["rstd"][:, :], q["var_eps"][:, :], minus_half[:, :],
                                            ALU.pow).then_inc(q["rstd_ready"], 1)
                return piece

            def apply(k):
                q = norm[k]

                def piece(g):
                    pool.wait_ge(q["var_ready"], g + 1)
                    earlier(pool, q["normed_ready"], g)
                    nc.gpsimd.tensor_tensor(q["centred"][:, :, :], q["src"][:, :, :],
                                            q["mean_var"][:, :, 0:1].broadcast_to([P, GB, D]),
                                            ALU.subtract).then_inc(q["centred_ready"], 1)
                    pool.wait_ge(q["centred_ready"], g + 1)
                    pool.wait_ge(q["rstd_ready"], g + 1)
                    earlier(pool, q["flipped"], g)
                    nc.gpsimd.tensor_tensor(q["normed"][:, :, :], q["centred"][:, :, :],
                                            wide(q["rstd"], D), ALU.mult).then_inc(q["normed_ready"], 1)
                return piece

            def f1_lo2(e):
                def piece(g):
                    pool.wait_ge(f1["hi2_ready"], nth(g, e, E1))
                    nc.gpsimd.tensor_tensor(f1["lo2"][e % 2][:, :], f1["gated"][e % 2][:, :],
                                            f1["hi2"][e % 2][:, :].bitcast(F32), ALU.subtract)\
                        .then_inc(f1["lo2_ready"], 1)
                return piece

            def add_bias(g):
                pool.wait_ge(f0["x_ready"], g + 1)
                earlier(pool, gnn["g1"]["x_ready"], g)
                nc.gpsimd.tensor_tensor(x2_bias[:, :, :], x2[:, :, :], every_graph(bias_g1, D),
                                        ALU.add).then_inc(x2_bias_ready, 1)

            def dst_parts(k):
                q = gnn[k]

                def piece(g):
                    dst, parts = q["src_dst"][:, :, 1], q["dst_parts"]
                    one = one_sb[:, :].broadcast_to([P, GB])
                    pool.wait_ge(q["src_dst_ready"], g + 1)
                    earlier(pool, q["rows_flipped"], g)
                    nc.gpsimd.tensor_tensor(parts[:, :, 0], dst, one, ALU.mult)\
                        .then_inc(q["part1_ready"], 1)
                    pool.wait_ge(q["part1_ready"], g + 1)
                    nc.gpsimd.tensor_tensor(q["rest1"][:, :], dst, parts[:, :, 0],
                                            ALU.subtract).then_inc(q["rest1_ready"], 1)
                    pool.wait_ge(q["rest1_ready"], g + 1)
                    nc.gpsimd.tensor_tensor(parts[:, :, 1], q["rest1"][:, :], one, ALU.mult)\
                        .then_inc(q["part2_ready"], 1)
                    pool.wait_ge(q["part2_ready"], g + 1)
                    nc.gpsimd.tensor_tensor(parts[:, :, 2], q["rest1"][:, :], parts[:, :, 1],
                                            ALU.subtract).then_inc(q["dst_parts_ready"], 1)
                return piece

            def gate_parts(g):
                a = p1["t6"]
                v = p1["parts"][:, :, :, 0:E1 * PARTS].rearrange("p b r (e k) -> p b r e k", k=PARTS)
                w = one_sb[:, :].unsqueeze(2).unsqueeze(3).broadcast_to([P, GB, REP, E1])

                def replicas(name):
                    return a[name][:, :, :].unsqueeze(2).broadcast_to([P, GB, REP, E1])

                pool.wait_ge(p1["link"], nth(g, 20, p1["LINKS"]))
                earlier(pool, p1["spread_flipped"], g)
                nc.gpsimd.tensor_tensor(v[:, :, :, :, 0], replicas("gates"), w, ALU.mult)\
                    .then_inc(p1["part_link"], 1)
                pool.wait_ge(p1["part_link"], nth(g, 0, 3))
                nc.gpsimd.tensor_tensor(a["rest1"][:, :, :], a["gates"][:, :, :], v[:, :, 0, :, 0],
                                        ALU.subtract).then_inc(p1["part_link"], 1)
                pool.wait_ge(p1["part_link"], nth(g, 1, 3))
                nc.gpsimd.tensor_tensor(v[:, :, :, :, 1], replicas("rest1"), w, ALU.mult)\
                    .then_inc(p1["part_link"], 1)
                pool.wait_ge(p1["part_link"], nth(g, 2, 3))
                nc.gpsimd.tensor_tensor(
                    v[:, :, :, :, 2], replicas("rest1"),
                    v[:, :, :, :, 1], ALU.subtract).then_inc(p1["parts_ready"], 1)

            def add_mixed(g):
                pool.wait_ge(mixed_relu_ready, g + 1)
                earlier(pool, norm["p0"]["normed_ready"], g)
                earlier(pool, x1_held_ready, g)
                nc.gpsimd.tensor_tensor(flat(x1), flat(x0), flat(mixed_relu),
                                        ALU.add).then_inc(gnn["g0"]["x_ready"], 1)

            def hold_x1(g):
                earlier(pool, f0["x_ready"], g)
                pool.wait_ge(gnn["g0"]["x_ready"], g + 1)
                nc.gpsimd.tensor_tensor(flat(x1_held), flat(x1), one_sb[:, :].broadcast_to([P, T]),
                                        ALU.mult).then_inc(x1_held_ready, 1)

            def hold_x3(g):
                earlier(pool, f1["x_ready"], g)
                pool.wait_ge(gnn["g1"]["x_ready"], g + 1)
                nc.gpsimd.tensor_tensor(flat(x3_held), flat(x3), one_sb[:, :].broadcast_to([P, T]),
                                        ALU.mult).then_inc(x3_held_ready, 1)

            def low_part(p):
                def piece(g):
                    pool.wait_ge(p["hi_ready"], g + 1)
                    pool.wait_ge(p["full_ready"], g + 1)
                    nc.gpsimd.tensor_tensor(p["lo"][:, :], p["full"][:, :], p["hi"][:, :].bitcast(F32),
                                            ALU.subtract).then_inc(p["lo_ready"], 1)
                return piece

            pieces = {"p0_lo": low_part(p0), "p1_lo": low_part(p1), "f1_hold": hold_x3,
                      "f0_hold": hold_x1, "g0_add": add_mixed,
                      "g1_bias": add_bias, "p1_parts": gate_parts}
            for k in ("g0", "p0"):
                pieces[f"{k}_apply"] = apply(k)
            for e in range(E1):
                pieces[f"f1_lo2_{e}"] = f1_lo2(e)
            for k in norm:
                pieces[f"{k}_rstd"] = rstd(k)
            for k in gnn:
                pieces[f"{k}_parts"] = dst_parts(k)
            run(pool, POOL_ORDER, pieces, [pick_expert], after=2)

        @block.scalar
        def _(act):
            for tile, src in first_loads:
                act.dma_start(tile, src).then_inc(first_in, 16)

            def gnn_flip(k):
                q = gnn[k]

                def piece(g):
                    act.wait_ge(norm[k]["flipped"], g + 1)
                    earlier(act, q["values_done"], g)
                    nc.scalar.activation(q["normed_t"][:, :], flip_bank[:, :], ACT.Copy)\
                        .then_inc(q["normed_t_ready"], 1)
                return piece

            def gnn_project(k):
                q = gnn[k]

                def piece(g):
                    act.wait_ge(q["src_dst_ready"], g + 1)
                    earlier(act, q["mixed"], g)
                    nc.scalar.activation(q["values"][:, 0:WIDE * D].rearrange("p (b d) -> p b d", d=D),
                                         value_cols[:, :, 0:D], ACT.Copy)
                    nc.scalar.activation(q["values"][:, WIDE * D:T], score_bank[:, 0:D], ACT.Copy)\
                        .then_inc(q["values_ready"], 1)
                return piece

            def gnn_softmax(k):
                q = gnn[k]

                def piece(g):
                    act.wait_ge(q["leaky_ready"], g + 1)
                    act.wait_ge(q["neg_leaky_max_ready"], g + 1)
                    earlier(act, q["probs_flipped"], g)
                    earlier(act, q["row_rcp_ready"], g)
                    for b in range(GB):
                        last = nc.scalar.activation(q["probs"][:, b, :], q["leaky"][:, b, :], ACT.Exp,
                                                    bias=q["neg_leaky_max"][:, b:b + 1],
                                                    accum_out=q["row_sum"][:, b:b + 1])
                    last.then_inc(q["probs_ready"], 1)
                return piece

            def gnn_probs_t(k):
                q = gnn[k]

                def piece(g):
                    act.wait_ge(q["probs_flipped"], g + 1)
                    earlier(act, q["mixed"], g)
                    nc.scalar.activation(q["probs_t"][:, :], flip_bank[:, :], ACT.Copy)\
                        .then_inc(q["probs_t_ready"], 1)
                return piece

            def g0_mix(g):
                q = gnn["g0"]
                act.wait_ge(q["mixed"], g + 1)
                act.wait_ge(q["row_rcp_ready"], g + 1)
                earlier(act, q["x_ready"], g)
                for b in range(GB):
                    last = nc.scalar.activation(mixed_relu[:, b, :], per_graph(value_bank, b), ACT.Relu,
                                                scale=q["row_rcp"][:, b:b + 1])
                last.then_inc(mixed_relu_ready, 1)

            def p_flip(k, p, last_read, n):
                def piece(g):
                    act.wait_ge(norm[k]["flipped"], g + 1)
                    earlier(act, last_read, g, 1, n - 1, n)
                    nc.scalar.activation(p["hi"][:, :], flip_bank[:, :], ACT.Copy).then_inc(p["hi_ready"], 1)
                return piece

            def p_full(k, p):
                def piece(g):
                    act.wait_ge(norm[k]["flipped"], g + 1)
                    earlier(act, p["lo_ready"], g)
                    if p is p0:
                        earlier(act, p0["logits_done"], g)
                    nc.scalar.activation(p["full"][:, :], flip_bank[:, :], ACT.Copy)\
                        .then_inc(p["full_ready"], 1)
                return piece

            def p0_spread(g):
                act.wait_ge(p0["spread_flipped"], g + 1)
                earlier(act, f0["up_done"], g, 1, CH - 1, CH)
                nc.scalar.activation(p0["spread"][:, :], flip16[:, 0:T], ACT.Copy).then_inc(p0["spread_ready"], 1)

            def p1_hidden(g):
                act.wait_ge(p1["hidden_done"], g + 1)
                earlier(act, p1["logits_done"], g)
                nc.scalar.activation(p1["hidden"][:, :], score_bank[:, :], ACT.Relu,
                                     bias=rt1_b[:, 0:1]).then_inc(p1["hidden_ready"], 1)

            def p1_exps(g):
                act.wait_ge(p1["link"], nth(g, 2, p1["LINKS"]))
                nc.scalar.activation(flat(p1["t6"]["exps"]), flat(p1["t6"]["shifted"]), ACT.Exp)\
                    .then_inc(p1["exps_ready"], 1)

            def p1_exp_next(g):
                act.wait_ge(p1["link"], nth(g, 7, p1["LINKS"]))
                nc.scalar.activation(p1["t1"]["exp_next"][:, :], p1["t1"]["next"][:, :], ACT.Exp)\
                    .then_inc(p1["exp_next_ready"], 1)

            def p1_exp_gap(g):
                act.wait_ge(p1["link"], nth(g, 14, p1["LINKS"]))
                nc.scalar.activation(p1["t1"]["exp_gap"][:, :], p1["t1"]["gap"][:, :], ACT.Exp)\
                    .then_inc(p1["exp_gap_ready"], 1)

            def p1_spread(g):
                act.wait_ge(p1["spread_flipped"], g + 1)
                earlier(act, f1["gate_done"], g, 1, E1 - 1, E1)
                nc.scalar.activation(p1["spread"][:, :], flip16[:, 0:T], ACT.Copy).then_inc(p1["spread_ready"], 1)

            def f0_chunk(c):
                def piece(g):
                    act.wait_ge(f0["up_done"], nth(g, c, CH))
                    if c >= 3:
                        act.wait_ge(f0["down_done"], nth(g, c - 3, CH))
                    else:
                        earlier(act, f0["down_done"], g, 1, CH - 1, CH)
                    nc.scalar.activation(f0["hi"][c % 3][:, :], f0_bank[c][:, :], ACT.Relu)\
                        .then_inc(f0["hi_ready"], 1)
                return piece

            def f0_tail(g):
                act.wait_ge(f0["down_done"], nth(g, CH - 1, CH))
                earlier(act, f0["sum_flipped"], g)
                nc.scalar.activation(f0["sum_t"][:, :], out_bank[:, :], ACT.Relu).then_inc(f0["sum_ready"], 1)

            def f1_relu1(e):
                def piece(g):
                    act.wait_ge(f1["up_done"], nth(g, e, E1))
                    if e >= 2:
                        act.wait_ge(f1["lo1_ready"], nth(g, e - 2, E1))
                    else:
                        earlier(act, f1["lo1_ready"], g, 1, E1 - 2 + e, E1)
                    nc.scalar.activation(f1["relu1"][e % 2][:, :], f1_up_bank[e][:, :], ACT.Relu,
                                         bias=b1_f1[:, e:e + 1]).then_inc(f1["relu1_ready"], 1)
                return piece

            def f1_hi1(e):
                def piece(g):
                    act.wait_ge(f1["up_done"], nth(g, e, E1))
                    if e >= 2:
                        act.wait_ge(f1["mid_done"], nth(g, e - 2, E1))
                    else:
                        earlier(act, f1["mid_done"], g, 1, E1 - 2 + e, E1)
                    nc.scalar.activation(f1["hi1"][e % 2][:, :], f1_up_bank[e][:, :], ACT.Relu,
                                         bias=b1_f1[:, e:e + 1]).then_inc(f1["hi1_ready"], 1)
                return piece

            def f1_hi2(e):
                def piece(g):
                    act.wait_ge(f1["gated_ready"], nth(g, e, E1))
                    if e >= 2:
                        act.wait_ge(f1["down_done"], nth(g, e - 2, E1))
                    else:
                        earlier(act, f1["down_done"], g, 1, E1 - 2 + e, E1)
                    nc.scalar.activation(f1["hi2"][e % 2][:, :], f1["gated"][e % 2][:, :], ACT.Copy)\
                        .then_inc(f1["hi2_ready"], 1)
                return piece

            def f1_relu2(e):
                def piece(g):
                    act.wait_ge(f1["mid_done"], nth(g, e, E1))
                    if e >= 2:
                        act.wait_ge(f1["gated_ready"], nth(g, e - 2, E1))
                    else:
                        earlier(act, f1["gated_ready"], g, 1, E1 - 2 + e, E1)
                    nc.scalar.activation(f1["relu2"][e % 2][:, :], f1_mid_bank[e][:, :],
                                         ACT.Relu, bias=b2_f1[:, e:e + 1])\
                        .then_inc(f1["relu2_ready"], 1)
                return piece

            def f1_tail(g):
                act.wait_ge(f1["down_done"], nth(g, E1 - 1, E1))
                earlier(act, f1["sum_flipped"], g)
                nc.scalar.activation(f1["sum_t"][:, :], out_bank[:, :], ACT.Copy).then_inc(f1["sum_ready"], 1)

            pieces = {"p0_full": p_full("p0", p0), "p1_full": p_full("p1", p1), "g0_relu": g0_mix,
                      "p0_hi": p_flip("p0", p0, f0["up_done"], CH),
                      "p1_hi": p_flip("p1", p1, f1["up_done"], E1), "p0_spread": p0_spread,
                      "p1_hidden": p1_hidden, "p1_exps": p1_exps, "p1_exp_next": p1_exp_next,
                      "p1_exp_gap": p1_exp_gap, "p1_spread": p1_spread, "t0_sum": f0_tail,
                      "f1_sum": f1_tail}
            for k in gnn:
                pieces[f"{k}_normed_t"] = gnn_flip(k)
                pieces[f"{k}_values"] = gnn_project(k)
                pieces[f"{k}_softmax"] = gnn_softmax(k)
                pieces[f"{k}_probs_t"] = gnn_probs_t(k)
            for c in range(CH):
                pieces[f"f0_hi{c}"] = f0_chunk(c)
            for e in range(E1):
                pieces[f"f1_relu1_{e}"] = f1_relu1(e)
                pieces[f"f1_hi1_{e}"] = f1_hi1(e)
                pieces[f"f1_relu2_{e}"] = f1_relu2(e)
                pieces[f"f1_hi2_{e}"] = f1_hi2(e)
            run(act, ACT_ORDER, pieces)

        @block.vector
        def _(dve):
            V = nc.vector
            dve.wait_ge(first_in, FIRST_LOADS)
            V.tensor_copy(ident16[:, :], ident[:, :])
            dve.wait_ge(score_w_done, 2)
            for n, k in enumerate(("g0", "g1")):
                last = V.tensor_copy(gnn[k]["w"][:, D:D + 2], value_bank[:, 2 * n:2 * n + 2])
            last.then_inc(setup_ready, 1)

            def split(n, name):
                def job():
                    dve.wait_ge(weights_in, LOADS)
                    V.tensor_copy(hi[name][:, :], raw[name][:, :]).then_inc(hi_split, 1)
                    dve.wait_ge(hi_split, n + 1)
                    V.tensor_tensor(lo[name][:, :], raw[name][:, :], hi[name][:, :].bitcast(F32),
                                    ALU.subtract).then_inc(lo_split, 1)
                return job

            def bias_part(name, r):
                full, stacked, part, done = bias_raw[name], bias16[name], part_tmp[name], part_done[name]
                rows = slice(KR * r, KR * (r + 1))

                def job():
                    dve.wait_ge(weights_in, LOADS)
                    dve.wait_ge(fills_done, 1)
                    if r > 0:
                        dve.wait_ge(done, 3 * r)
                    V.tensor_copy(part[:, :], full[:, :]).then_inc(done, 1)
                    dve.wait_ge(done, 3 * r + 1)
                    V.tensor_copy(stacked[rows, :], part[rows, :]).then_inc(done, 1)
                    if r < PARTS - 1:
                        dve.wait_ge(done, 3 * r + 2)
                        V.tensor_tensor(full[:, :], full[:, :], part[:, :], ALU.subtract).then_inc(done, 1)
                return job

            def copy_pick():
                dve.wait_ge(weights_in, LOADS)
                V.tensor_copy(pick16[:, :, :], pick_f32[:, :, :]).then_inc(lo_split, 1)

            def stats(k):
                q = norm[k]
                source_ready = {"g0": (x_in, 16), "p0": (gnn["g0"]["x_ready"], 1), "g1": (f0["x_ready"], 1),
                                "p1": (gnn["g1"]["x_ready"], 1)}[k]

                def piece(g):
                    dve.wait_ge(source_ready[0], (g + 1) * source_ready[1])
                    earlier(dve, q["normed_ready"], g)
                    for b in range(GB):
                        last = V.bn_stats(q["stats"][:, b, :], q["src"][:, b, :])
                    last.then_inc(q["stats_done"], 1)
                return piece

            def aggregate(k):
                q = norm[k]

                def piece(g):
                    count = g + 1
                    apart(dve)
                    dve.wait_ge(q["stats_done"], count)
                    for b in range(GB):
                        last = V.bn_aggr(q["mean_var"][:, b, :], q["stats"][:, b, :])
                    last.then_inc(q["var_ready"], 1)
                return piece

            def apply(k):
                q = norm[k]

                def piece(g):
                    dve.wait_ge(q["rstd_ready"], g + 1)
                    earlier(dve, q["flipped"], g)
                    for b in range(GB):
                        last = V.tensor_scalar(q["normed"][:, b, :], q["src"][:, b, :],
                                               q["mean_var"][:, b, 0:1], q["rstd"][:, b:b + 1],
                                               ALU.subtract, ALU.mult)
                    last.then_inc(q["normed_ready"], 1)
                return piece

            def mask(k):
                q = gnn[k]

                def piece(g):
                    dve.wait_ge(q["adj_in"], 16 * (g + 1))
                    earlier(dve, q["scores_ready"], g)
                    V.tensor_scalar(q["masked"][:, :], flat(q["adj"]), 0.0, NEG_BIG, ALU.is_le,
                                    ALU.mult).then_inc(q["mask_ready"], 1)
                return piece

            def gnn_src_dst(k):
                q = gnn[k]

                def piece(g):
                    dve.wait_ge(q["values_done"], g + 1)
                    earlier(dve, q["scores_ready"], g)
                    earlier(dve, q["dst_parts_ready"], g)
                    V.tensor_copy(q["src_dst"][:, 0:WIDE, :], value_cols[:, :, D:D + 2])
                    V.tensor_copy(q["src_dst"][:, WIDE, :], score_bank[:, D:D + 2])\
                        .then_inc(q["src_dst_ready"], 1)
                return piece

            def gnn_row(k):
                q = gnn[k]

                def piece(g):
                    dve.wait_ge(q["rows_flipped"], g + 1)
                    V.tensor_copy(q["dst_rows"][:, :], flip16[0:KR, 0:T]).then_inc(q["rows_ready"], 1)
                return piece

            def gnn_scores(k):
                q = gnn[k]

                def piece(g):
                    dve.wait_ge(q["scores_done"], g + 1)
                    dve.wait_ge(q["src_dst_ready"], g + 1)
                    dve.wait_ge(q["mask_ready"], g + 1)
                    earlier(dve, q["leaky_ready"], g)
                    for b in range(GB):
                        last = V.scalar_tensor_tensor(q["scores"][:, b, :], per_graph(score_bank, b),
                                                      q["src_dst"][:, b, 0:1], per_graph(q["masked"], b),
                                                      ALU.add, ALU.add)
                    last.then_inc(q["scores_ready"], 1)
                return piece

            def gnn_leaky(k):
                q = gnn[k]

                def piece(g):
                    dve.wait_ge(q["scores_ready"], g + 1)
                    V.tensor_reduce(q["neg_max"][:, :], q["scores"][:, :, :], AX_X, ALU.max, negate=True)\
                        .then_inc(q["neg_max_ready"], 1)
                    V.scalar_tensor_tensor(flat(q["leaky"]), flat(q["scores"]), SLOPE, flat(q["scores"]),
                                           ALU.mult, ALU.max).then_inc(q["leaky_ready"], 1)
                    dve.wait_ge(q["neg_max_ready"], g + 1)
                    V.scalar_tensor_tensor(q["neg_leaky_max"][:, :], q["neg_max"][:, :], SLOPE, q["neg_max"][:, :],
                                           ALU.mult, ALU.min).then_inc(q["neg_leaky_max_ready"], 1)
                return piece

            def gnn_row_rcp(k):
                q = gnn[k]

                def piece(g):
                    dve.wait_ge(q["probs_ready"], g + 1)
                    earlier(dve, mixed_relu_ready if k == "g0" else q["x_ready"], g)
                    V.reciprocal(q["row_rcp"][:, :], q["row_sum"][:, :]).then_inc(q["row_rcp_ready"], 1)
                return piece

            def g1_mix(g):
                q = gnn["g1"]
                dve.wait_ge(q["mixed"], g + 1)
                dve.wait_ge(x2_bias_ready, g + 1)
                dve.wait_ge(q["row_rcp_ready"], g + 1)
                earlier(dve, norm["p1"]["normed_ready"], g)
                earlier(dve, x3_held_ready, g)
                for b in range(GB):
                    last = V.scalar_tensor_tensor(x3[:, b, :], per_graph(value_bank, b),
                                                  q["row_rcp"][:, b:b + 1], x2_bias[:, b, :],
                                                  ALU.mult, ALU.add)
                last.then_inc(q["x_ready"], 1)

            def p0_route(i):
                def piece(g):
                    logits, at_top, ranked = (p0[n][:, :, :] for n in ("logits", "at_top", "ranked"))
                    if i > 0:
                        dve.wait_ge(p0["link"], nth(g, i - 1, p0["LINKS"]))
                    if i == 0:
                        dve.wait_ge(p0["logits_done"], g + 1)
                        ins = V.tensor_tensor(
                            logits, score_bank[:, 0:GB * E0].rearrange("p (b e) -> p b e", e=E0),
                            every_graph(rt0_b, E0), ALU.add)
                    if i == 1:
                        ins = V.tensor_reduce(p0["top"][:, :], logits, AX_X, ALU.max)
                    if i == 2:
                        ins = V.tensor_tensor(at_top, logits, wide(p0["top"], E0), ALU.is_equal)
                    if i == 3:
                        ins = V.tensor_tensor(ranked, at_top, every_graph(rank0_sb, E0), ALU.mult)
                    if i == 4:
                        ins = V.tensor_reduce(p0["first"][:, :], ranked, AX_X, ALU.max)
                    if i == 5:
                        earlier(dve, p0["spread_flipped"], g)
                        V.tensor_tensor(
                            p0["onehot"][:, :, :, :], ranked.unsqueeze(2).broadcast_to([P, GB, REP, E0]),
                            p0["first"][:, :].unsqueeze(2).unsqueeze(3).broadcast_to([P, GB, REP, E0]),
                            ALU.is_equal).then_inc(p0["onehot_ready"], 1)
                    else:
                        ins.then_inc(p0["link"], 1)
                return piece

            def p1_route(i):
                a, c = p1["t6"], p1["t1"]
                rank = every_graph(rank1_sb, E1)

                def full(name):
                    return a[name][:, :, :]

                def per_token(name):
                    return wide(c[name], E1)

                def piece(g):
                    if i > 0:
                        dve.wait_ge(p1["link"], nth(g, i - 1, p1["LINKS"]))
                    if i == 0:
                        dve.wait_ge(p1["logits_done"], g + 1)
                        ins = V.tensor_tensor(
                            full("logits"), score_bank[:, 0:GB * E1].rearrange("p (b e) -> p b e", e=E1),
                            every_graph(rt2_b, E1), ALU.add)
                    if i == 1:
                        ins = V.tensor_reduce(c["neg_max"][:, :], full("logits"), AX_X, ALU.max,
                                              negate=True)
                    if i == 2:
                        earlier(dve, p1["exps_ready"], g)
                        ins = V.tensor_tensor(full("shifted"), full("logits"), per_token("neg_max"),
                                              ALU.add)
                    if i == 3:
                        ins = V.scalar_tensor_tensor(full("ranked"), full("shifted"), 0.0, rank,
                                                     ALU.is_equal, ALU.mult)
                    if i == 4:
                        ins = V.tensor_reduce(c["rank_top"][:, :], full("ranked"), AX_X, ALU.max)
                    if i == 5:
                        ins = V.tensor_tensor(full("first"), full("ranked"), per_token("rank_top"),
                                              ALU.is_equal)
                    if i == 6:
                        ins = V.scalar_tensor_tensor(full("others"), full("first"), UNSELECTED,
                                                     full("shifted"), ALU.mult, ALU.add)
                    if i == 7:
                        earlier(dve, p1["exp_next_ready"], g)
                        ins = V.tensor_reduce(c["next"][:, :], full("others"), AX_X, ALU.max)
                    if i == 8:
                        ins = V.tensor_tensor(full("at_second"), full("others"), per_token("next"),
                                              ALU.is_equal)
                    if i == 9:
                        ins = V.tensor_tensor(full("ranked2"), full("at_second"), rank, ALU.mult)
                    if i == 10:
                        ins = V.tensor_reduce(c["rank_next"][:, :], full("ranked2"), AX_X, ALU.max)
                    if i == 11:
                        ins = V.tensor_tensor(full("second"), full("ranked2"), per_token("rank_next"),
                                              ALU.is_equal)
                    if i == 12:
                        dve.wait_ge(p1["exps_ready"], g + 1)
                        ins = V.tensor_reduce(c["sum"][:, :], full("exps"), AX_X, ALU.add)
                    if i == 13:
                        ins = V.reciprocal(c["rcp"][:, :], c["sum"][:, :])
                    if i == 14:
                        dve.wait_ge(p1["exp_next_ready"], g + 1)
                        earlier(dve, p1["exp_gap_ready"], g)
                        ins = V.scalar_tensor_tensor(c["gap"][:, :], c["exp_next"][:, :], -1.0,
                                                     c["rcp"][:, :], ALU.add, ALU.mult)
                    if i == 15:
                        dve.wait_ge(p1["exp_gap_ready"], g + 1)
                        ins = V.tensor_scalar(c["gap_sum"][:, :], c["exp_gap"][:, :], 1.0, None, ALU.add)
                    if i == 16:
                        ins = V.reciprocal(c["weight1"][:, :], c["gap_sum"][:, :])
                    if i == 17:
                        ins = V.tensor_tensor(c["weight2"][:, :], c["exp_gap"][:, :], c["weight1"][:, :],
                                              ALU.mult)
                    if i == 18:
                        ins = V.tensor_tensor(full("gate1"), full("first"), per_token("weight1"), ALU.mult)
                    if i == 19:
                        ins = V.tensor_tensor(full("gate2"), full("second"), per_token("weight2"),
                                              ALU.mult)
                    if i == 20:
                        earlier(dve, p1["parts_ready"], g)
                        ins = V.tensor_tensor(full("gates"), full("gate1"), full("gate2"), ALU.add)
                    ins.then_inc(p1["link"], 1)
                return piece

            def f0_chunk(c):
                def piece(g):
                    dve.wait_ge(f0["hi_ready"], nth(g, c, CH))
                    V.scalar_tensor_tensor(f0["lo"][c % 3][:, :], f0_bank[c][:, :], 0.0,
                                           f0["hi"][c % 3][:, :].bitcast(F32), ALU.max,
                                           ALU.subtract).then_inc(f0["lo_ready"], 1)
                return piece

            def f0_tail(g):
                dve.wait_ge(f0["sum_flipped"], g + 1)
                dve.wait_ge(x1_held_ready, g + 1)
                earlier(dve, norm["g1"]["normed_ready"], g)
                earlier(dve, x2_bias_ready, g)
                V.tensor_tensor(flat(x2), flat(x1_held), gate_bank[:, :], ALU.add).then_inc(f0["x_ready"], 1)

            def f1_lo1(e):
                def piece(g):
                    dve.wait_ge(f1["relu1_ready"], nth(g, e, E1))
                    dve.wait_ge(f1["hi1_ready"], nth(g, e, E1))
                    V.tensor_tensor(f1["lo1"][e % 2][:, :], f1["relu1"][e % 2][:, :],
                                    f1["hi1"][e % 2][:, :].bitcast(F32), ALU.subtract)\
                        .then_inc(f1["lo1_ready"], 1)
                return piece

            def f1_gated(e):
                def piece(g):
                    dve.wait_ge(f1["relu2_ready"], nth(g, e, E1))
                    dve.wait_ge(f1["gate_done"], nth(g, e, E1))
                    if e >= 2:
                        dve.wait_ge(f1["lo2_ready"], nth(g, e - 2, E1))
                    else:
                        earlier(dve, f1["lo2_ready"], g, 1, E1 - 2 + e, E1)
                    V.tensor_tensor(f1["gated"][e % 2][:, :], f1["relu2"][e % 2][:, :], gate_bank[:, :],
                                    ALU.mult).then_inc(f1["gated_ready"], 1)
                return piece

            def f1_tail(g):
                dve.wait_ge(f1["sum_flipped"], g + 1)
                dve.wait_ge(x3_held_ready, g + 1)
                if not isinstance(g, int) or g >= 1:
                    dve.wait_ge(x_out, 16 * g)
                V.tensor_tensor(flat(x4), flat(x3_held), gate_bank[:, :], ALU.add).then_inc(f1["x_ready"], 1)

            pieces = {"g0_mask": mask("g0"), "g1_mask": mask("g1"), "g1_add": g1_mix, 
                      "t0_add": f0_tail, "f1_add": f1_tail}
            for k in norm:
                pieces[f"{k}_stats"] = stats(k)
                pieces[f"{k}_aggregate"] = aggregate(k)
            for k in ("g1", "p1"):
                pieces[f"{k}_apply"] = apply(k)
            for k in gnn:
                pieces[f"{k}_src_dst"] = gnn_src_dst(k)
                pieces[f"{k}_rows"] = gnn_row(k)
                pieces[f"{k}_scores"] = gnn_scores(k)
                pieces[f"{k}_leaky"] = gnn_leaky(k)
                pieces[f"{k}_row_rcp"] = gnn_row_rcp(k)
            for i in range(p0["LINKS"] + 1):
                pieces[f"p0_route{i}"] = p0_route(i)
            for i in range(p1["LINKS"]):
                pieces[f"p1_route{i}"] = p1_route(i)
            for c in range(CH):
                pieces[f"f0_lo{c}"] = f0_chunk(c)
            for e in range(E1):
                pieces[f"f1_lo1_{e}"] = f1_lo1(e)
                pieces[f"f1_gated_{e}"] = f1_gated(e)
            b1_jobs = [bias_part("b1_f0", r) for r in range(PARTS)]
            b2_jobs = [bias_part("b2_f0", r) for r in range(PARTS)]
            b3_jobs = [bias_part("b3_f1", r) for r in range(PARTS)]
            splits = [split(n, name) for n, name in enumerate(split_sources)]

            def together(jobs):
                def job():
                    for j in jobs:
                        j()
                return job

            jobs = b1_jobs + [together(splits[:2] + b2_jobs)]
            jobs += splits[2:] + [together(b3_jobs), copy_pick]
            run(dve, DVE_ORDER, pieces, jobs, after=3)

        @block.tensor
        def _(pe):
            M = nc.tensor.matmul

            def three(bank, w, cols, x_hi, x_lo, start, stop):
                M(bank[:, :], hi[w][:, cols], x_hi[:, :], start=start, stop=False)
                M(bank[:, :], hi[w][:, cols], x_lo[:, :], start=False, stop=False)
                return M(bank[:, :], lo[w][:, cols], x_hi[:, :], start=False, stop=stop)

            def columns(n):
                return slice(n * P, (n + 1) * P)

            pe.wait_ge(first_in, FIRST_LOADS)
            for n, k in enumerate(("g0", "g1")):
                M(value_bank[:, 2 * n:2 * n + 2], gnn[k]["w_turned"][:, :], gnn[k]["a"][:, :], start=True,
                  stop=True).then_inc(score_w_done, 1)
            pe.wait_ge(setup_ready, 1)

            def weights_ready(g, splits, bias):
                if isinstance(g, int) and g == 0:
                    pe.wait_ge(lo_split, splits)
                    pe.wait_ge(picked, PARTS)
                    pe.wait_ge(part_done[bias], BIAS_STEPS)

            def flip(k):
                q = norm[k]

                def piece(g):
                    pe.wait_ge(q["normed_ready"], g + 1)
                    turn(f"{k}_flip", g)
                    for b in range(GB):
                        last = nc.tensor.transpose(per_graph(flip_bank, b), q["normed"][:, b, :], ident[:, :])
                    last.then_inc(q["flipped"], 1)
                return piece

            turns = {
                "g1_flip_probs": [[(p1["spread_ready"], -1, 0, 1),
                                   (gnn["g1"]["rows_ready"], 0, 0, 1)]],
                "p0_flip": [[(gnn["g1"]["probs_t_ready"], -2, 0, 1),
                             (p1["spread_ready"], -3, 0, 1),
                             (gnn["g0"]["probs_t_ready"], 0, 0, 1)]],
                "p0_route": [[(gnn["g1"]["scores_ready"], -2, 0, 1),
                              (p1["link"], -3, 0, 21),
                              (gnn["g0"]["scores_ready"], 0, 0, 1)]],
                "g0_flip": [[(p0["full_ready"], -1, 0, 1),
                             (gnn["g1"]["probs_t_ready"], -3, 0, 1),
                             (p1["spread_ready"], -4, 0, 1)]],
                "g0_project": [[(p0["link"], -1, 0, 5),
                                (gnn["g1"]["scores_ready"], -3, 0, 1),
                                (p1["link"], -4, 0, 21)],
                               [(gnn["g1"]["x_ready"], -3, 0, 1),
                                (mixed_relu_ready, -1, 0, 1)]],
                "p0_turn": [[(gnn["g0"]["rows_ready"], 1, 0, 1),
                             (p0["full_ready"], 0, 0, 1)]],
                "g0_score": [[(gnn["g0"]["values_ready"], 0, 0, 1)]],
                "p1_flip": [[(p0["spread_ready"], 2, 0, 1),
                             (gnn["g0"]["rows_ready"], 3, 0, 1),
                             (gnn["g1"]["probs_t_ready"], 0, 0, 1)]],
                "p1_hide": [[(gnn["g0"]["scores_ready"], 3, 0, 1),
                             (p0["link"], 2, 0, 5),
                             (gnn["g1"]["scores_ready"], 0, 0, 1)]],
                "g0_flip_probs": [[(p1["full_ready"], -3, 0, 1),
                                   (p0["spread_ready"], -1, 0, 1),
                                   (gnn["g0"]["rows_ready"], 0, 0, 1)]],
                "g1_flip": [[(gnn["g0"]["probs_t_ready"], 2, 0, 1),
                             (p1["full_ready"], -1, 0, 1),
                             (p1["spread_ready"], -2, 0, 1)]],
                "g1_project": [[(p1["link"], -1, 0, 21),
                                (gnn["g0"]["scores_ready"], 2, 0, 1)],
                               [(mixed_relu_ready, 2, 0, 1),
                                (gnn["g1"]["x_ready"], -1, 0, 1)]],
                "g1_score": [[(gnn["g1"]["values_ready"], 0, 0, 1)]],
                "p1_turn": [[(gnn["g1"]["rows_ready"], 1, 0, 1),
                             (gnn["g0"]["probs_t_ready"], 3, 0, 1),
                             (p1["full_ready"], 0, 0, 1)]],
            }

            def turn(name, g):
                for last_pieces in turns.get(name, []):
                    for signal, by, i, n in last_pieces:
                        if not isinstance(g, int) or 0 <= g + by < GROUPS:
                            pe.wait_ge(signal, nth(g + by, i, n))
                            break

            def gnn_project(k):
                q = gnn[k]

                def piece(g):
                    pe.wait_ge(q["normed_t_ready"], g + 1)
                    turn(f"{k}_project", g)
                    for b in range(GB):
                        cols = value_cols[:, b, :] if b < WIDE else score_bank[:, 0:D + 2]
                        last = M(cols, per_graph(q["normed_t"], b), q["w"][:, :], start=True, stop=True)
                    last.then_inc(q["values_done"], 1)
                return piece

            def gnn_row(k):
                q = gnn[k]

                def piece(g):
                    pe.wait_ge(q["dst_parts_ready"], g + 1)
                    turn(f"{k}_row", g)
                    for b in range(GB):
                        last = nc.tensor.transpose(flip16[0:KR, b * N:(b + 1) * N], q["dst_parts"][:, b, :],
                                                   ident16[:, :])
                    last.then_inc(q["rows_flipped"], 1)
                return piece

            def gnn_scores(k):
                q = gnn[k]

                def piece(g):
                    pe.wait_ge(q["rows_ready"], g + 1)
                    turn(f"{k}_score", g)
                    M(score_bank[:, :], ones16[:, :], q["dst_rows"][:, :], start=True, stop=True)\
                        .then_inc(q["scores_done"], 1)
                return piece

            def gnn_flip_probs(k):
                q = gnn[k]

                def piece(g):
                    pe.wait_ge(q["probs_ready"], g + 1)
                    turn(f"{k}_flip_probs", g)
                    for b in range(GB):
                        last = nc.tensor.transpose(per_graph(flip_bank, b), q["probs"][:, b, :], ident[:, :])
                    last.then_inc(q["probs_flipped"], 1)
                return piece

            def gnn_mix(k):
                q = gnn[k]

                def piece(g):
                    pe.wait_ge(q["probs_t_ready"], g + 1)
                    pe.wait_ge(q["values_ready"], g + 1)
                    turn(f"{k}_mix", g)
                    for b in range(GB):
                        last = M(per_graph(value_bank, b), per_graph(q["probs_t"], b), per_graph(q["values"], b),
                                 start=True, stop=True)
                    last.then_inc(q["mixed"], 1)
                return piece

            def p0_route(g):
                if isinstance(g, int) and g == 0:
                    pe.wait_ge(weights_in, LOADS)
                pe.wait_ge(p0["full_ready"], g + 1)
                turn("p0_route", g)
                for b in range(GB):
                    out_cols = score_bank[:, b * E0:(b + 1) * E0]
                    last = M(out_cols, per_graph(p0["full"], b), rt0[:, :], start=True, stop=True)
                last.then_inc(p0["logits_done"], 1)

            def p0_spread(g):
                pe.wait_ge(p0["onehot_ready"], g + 1)
                turn("p0_turn", g)
                for b in range(GB):
                    last = nc.tensor.transpose(flip16[:, b * N:(b + 1) * N],
                                               p0["onehot"][:, b, :, :].rearrange("p r e -> p (r e)"),
                                               ident16[:, :])
                last.then_inc(p0["spread_flipped"], 1)

            def p1_hidden(g):
                weights_ready(g, NSPLIT + 1, "b3_f1")
                pe.wait_ge(p1["lo_ready"], g + 1)
                turn("p1_hide", g)
                three(score_bank, "rt1", columns(0), p1["hi"], p1["lo"], True, True).then_inc(p1["hidden_done"], 1)

            def p1_route(g):
                pe.wait_ge(p1["hidden_ready"], g + 1)
                turn("p1_route", g)
                for b in range(GB):
                    last = M(score_bank[:, b * E1:(b + 1) * E1], per_graph(p1["hidden"], b), rt2[:, :],
                             start=True, stop=True)
                last.then_inc(p1["logits_done"], 1)

            def p1_spread(g):
                pe.wait_ge(p1["parts_ready"], g + 1)
                turn("p1_turn", g)
                for b in range(GB):
                    last = nc.tensor.transpose(flip16[:, b * N:(b + 1) * N],
                                               p1["parts"][:, b, :, :].rearrange("p r k -> p (r k)"),
                                               ident16[:, :])
                last.then_inc(p1["spread_flipped"], 1)

            def f0_up(c):
                def piece(g):
                    if c == 0:
                        weights_ready(g, 2, "b2_f0")
                        pe.wait_ge(p0["lo_ready"], g + 1)
                        pe.wait_ge(p0["spread_ready"], g + 1)
                    if c >= 3:
                        pe.wait_ge(f0["lo_ready"], nth(g, c - 3, CH))
                    else:
                        reached(pe, f1["relu2_ready"], g, -F1_BEHIND, E1 - 3 + c, E1)
                    M(f0_bank[c][:, :], bias16["b1_f0"][:, columns(c)], p0["spread"][:, :],
                      start=True, stop=False)
                    three(f0_bank[c], "w1_f0", columns(c), p0["hi"], p0["lo"], False, True)\
                        .then_inc(f0["up_done"], 1)
                return piece

            def f0_down(c):
                def piece(g):
                    if c == 0:
                        reached(pe, f1["sum_ready"], g, -F1_BEHIND)
                        M(out_bank[:, :], bias16["b2_f0"][:, :], p0["spread"][:, :], start=True,
                          stop=False)
                    pe.wait_ge(f0["lo_ready"], nth(g, c, CH))
                    three(out_bank, "w2_f0", columns(c), f0["hi"][c % 3], f0["lo"][c % 3], False,
                          c == CH - 1).then_inc(f0["down_done"], 1)
                return piece

            def tail(f):
                def piece(g):
                    pe.wait_ge(f["sum_ready"], g + 1)
                    if f is f0:
                        reached(pe, f1["x_ready"], g, -F1_BEHIND)
                    for b in range(GB):
                        last = nc.tensor.transpose(per_graph(gate_bank, b), per_graph(f["sum_t"], b),
                                                   ident[:, :])
                    last.then_inc(f["sum_flipped"], 1)
                return piece

            def f1_up(e):
                def piece(g):
                    if e == 0:
                        pe.wait_ge(p1["spread_ready"], g + 1)
                    if e < 2:
                        reached(pe, f0["lo_ready"], g, F1_BEHIND - 1, CH - 3 + 2 * e, CH)
                    three(f1_up_bank[e], "w1_f1", columns(e), p1["hi"], p1["lo"], True, True)\
                        .then_inc(f1["up_done"], 1)
                return piece

            def f1_mid(e):
                def piece(g):
                    if e == 0:
                        reached(pe, f0["x_ready"], g, F1_BEHIND - 1)
                        if isinstance(g, int):
                            earlier(pe, f1["x_ready"], g)
                    else:
                        pe.wait_ge(f1["gated_ready"], nth(g, e - 1, E1))
                    M(gate_bank[:, :], pick16[:, e, :], p1["spread"][:, :], start=True, stop=True)\
                        .then_inc(f1["gate_done"], 1)
                    pe.wait_ge(f1["lo1_ready"], nth(g, e, E1))
                    three(f1_mid_bank[e], "w2_f1", columns(e), f1["hi1"][e % 2], f1["lo1"][e % 2],
                          True, True).then_inc(f1["mid_done"], 1)
                return piece

            def f1_down(e):
                def piece(g):
                    if e == 0:
                        reached(pe, f0["sum_ready"], g, F1_BEHIND - 1)
                        M(out_bank[:, :], bias16["b3_f1"][:, :], p1["spread"][:, :], start=True, stop=False)
                    pe.wait_ge(f1["lo2_ready"], nth(g, e, E1))
                    three(out_bank, "w3_f1", columns(e), f1["hi2"][e % 2], f1["lo2"][e % 2], False,
                          e == E1 - 1).then_inc(f1["down_done"], 1)
                return piece

            pieces = {"g0_flip": flip("g0"), "g1_flip": flip("g1"),
                      "p0_flip": flip("p0"), "p1_flip": flip("p1"),
                      "p0_route": p0_route, "p0_turn": p0_spread, "p1_hide": p1_hidden,
                      "p1_route": p1_route, "p1_turn": p1_spread, "t0_turn": tail(f0),
                      "f1_turn": tail(f1)}
            for k in gnn:
                pieces[f"{k}_project"] = gnn_project(k)
                pieces[f"{k}_row"] = gnn_row(k)
                pieces[f"{k}_score"] = gnn_scores(k)
                pieces[f"{k}_flip_probs"] = gnn_flip_probs(k)
                pieces[f"{k}_mix"] = gnn_mix(k)
            for c in range(CH):
                pieces[f"f0_up{c}"] = f0_up(c)
                pieces[f"f0_down{c}"] = f0_down(c)
            for e in range(E1):
                pieces[f"f1_up{e}"] = f1_up(e)
                pieces[f"f1_mid{e}"] = f1_mid(e)
                pieces[f"f1_down{e}"] = f1_down(e)
            run(pe, PE_ORDER, pieces)


def kernel(x, adj, L0_gnn_W, L0_gnn_a, L0_ffn_router_w, L0_ffn_router_b, L0_ffn_W1, L0_ffn_b1, L0_ffn_W2,
           L0_ffn_b2, L1_gnn_W, L1_gnn_a, L1_gnn_bias, L1_ffn_router_w1, L1_ffn_router_b1,
           L1_ffn_router_w2, L1_ffn_router_b2, L1_ffn_expert_w1, L1_ffn_expert_b1, L1_ffn_expert_w2,
           L1_ffn_expert_b2, L1_ffn_expert_w3, L1_ffn_expert_b3):
    import numpy as np
    import concourse.bacc as bacc
    from concourse import mybir as mb
    from concourse.bass_utils import run_bass_kernel_spmd

    D = x.shape[2]
    E0, E1, R1 = L0_ffn_router_w.shape[0], L1_ffn_router_w2.shape[1], L1_ffn_router_w1.shape[1]
    REP, KR, PARTS = 4, 32, 3

    def widened(a, shape):
        out = np.zeros(shape, a.dtype)
        out[tuple(slice(0, n) for n in a.shape)] = a
        return out

    def experts_inside(w):
        return w.transpose(1, 0, 2).reshape(w.shape[1], -1)

    pick = np.zeros((128, E1, 128), np.float32)
    for e in range(E1):
        pick[e * PARTS:(e + 1) * PARTS, e, :] = 1.0
    ins = {
        "x": x, "adj": adj,
        "g0_w": L0_gnn_W, "g0_w_turned": L0_gnn_W.T, "g0_a": L0_gnn_a.reshape(2, D).T,
        "g1_w": L1_gnn_W.T, "g1_w_turned": L1_gnn_W, "g1_a": L1_gnn_a.T, "g1_bias": L1_gnn_bias,
        "f0_router": L0_ffn_router_w.T, "f0_router_b": L0_ffn_router_b,
        "f0_w1": experts_inside(L0_ffn_W1), "f0_b1": L0_ffn_b1.reshape(-1),
        "f0_w2": L0_ffn_W2.reshape(-1, D), "f0_b2": np.tile(L0_ffn_b2, (REP, 1)),
        "f1_router1": widened(L1_ffn_router_w1, (D, 128)),
        "f1_router1_b": widened(L1_ffn_router_b1.reshape(R1, 1), (128, 1)),
        "f1_router2": widened(L1_ffn_router_w2, (128, E1)), "f1_router2_b": L1_ffn_router_b2,
        "f1_w1": experts_inside(L1_ffn_expert_w1), "f1_b1": L1_ffn_expert_b1.T,
        "f1_w2": experts_inside(L1_ffn_expert_w2), "f1_b2": L1_ffn_expert_b2.T,
        "f1_w3": experts_inside(L1_ffn_expert_w3),
        "f1_b3": np.tile(widened(np.repeat(L1_ffn_expert_b3, PARTS, axis=0), (KR, D)), (REP, 1)),
        "eye": np.eye(128, dtype=np.float32),
        "rank0": np.tile(np.arange(E0, 0, -1, dtype=np.float32), (128, 1)),
        "rank1": np.tile(np.arange(E1, 0, -1, dtype=np.float32), (128, 1)),
        "gate_pick": pick,
    }
    nc = bacc.Bacc("TRN2", target_bir_lowering=False, num_devices=1)
    arrays, args = {}, []
    for name, a in ins.items():
        arrays[f"in_{name}"] = np.ascontiguousarray(a)
        args.append(nc.dram_tensor(f"in_{name}", a.shape, mb.dt.from_np(a.dtype), kind="ExternalInput").ap())
    args.append(nc.dram_tensor("out_x", x.shape, mb.dt.from_np(x.dtype), kind="ExternalOutput").ap())
    four_layer_kernel(nc, *args)
    return run_bass_kernel_spmd(nc, [arrays], core_ids=[0]).results[0]["out_x"]
```
